# Optimizing a Trainium2 kernel written in Bass

```python
import numpy as np
import jax
import jax.numpy as jnp

def _softmax(x, axis=-1):
    return jax.nn.softmax(x, axis=axis)

def _gelu(x):
    return jax.nn.gelu(x, approximate=True)

def _silu(x):
    return jax.nn.silu(x)

def _sigmoid(x):
    return jax.nn.sigmoid(x)

def _layernorm(x, axis=-1, eps=1e-05):
    m = jnp.mean(x, axis=axis, keepdims=True)
    v = jnp.var(x, axis=axis, keepdims=True)
    return (x - m) / jnp.sqrt(v + eps)

def _scatter_add(tgt, idx, src, axis=0):
    return tgt.at[idx].add(src)

def _segment_sum(src, seg, n):
    return jax.ops.segment_sum(src, seg, n)
kernel_name = 'mk_vit_tower_d1_tok_img1024_r4_d5178e'

def setup_inputs(seed: int=0):
    np.random.seed(seed)
    _w = jnp.asarray

    def _rec_inputs():
        import jax
        import jax.numpy as jnp
        _rk = jax.random.key(seed)
        x = -0.000125008 + 0.999885 * jax.random.normal(jax.random.fold_in(_rk, 1), (4, 512, 256, 4), jnp.float32)
        return x
    x = _rec_inputs()

    def _L0_tok_setup():
        import jax, jax.numpy as jnp
        import numpy as np
        key = jax.random.key(seed)
        k1, k2, k3 = jax.random.split(key, 3)
        B, H, I, O, Dp1 = (4, 512, 256, 256, 4)
        x = jax.random.normal(k1, (B, H, I, Dp1), dtype=jnp.float32)
        weight = 0.1 * jax.random.normal(k2, (O, Dp1), dtype=jnp.float32)
        weighted_sum = 0.1 * jax.random.normal(k3, (O, I), dtype=jnp.float32)
        return {'x': x, 'weight': weight, 'weighted_sum': weighted_sum}
    _L0_tok_all = _L0_tok_setup()
    _L0_tok_in = {k: v for k, v in _L0_tok_all.items() if k in ('weight', 'weighted_sum')}
    del _L0_tok_all

    def _L0_attn_setup():
        import jax, jax.numpy as jnp
        import numpy as np
        DIM = 256
        HEADS = 16
        HEAD_DIM = DIM // HEADS
        K = 13
        NS = K // 2
        SCALE = HEAD_DIM ** (-0.5)
        key = jax.random.key(seed)
        ks = jax.random.split(key, 5)
        B, L = (2, 1024)
        x = jax.random.normal(ks[0], (B, L, DIM), jnp.float32)
        qkv_w = jax.random.normal(ks[1], (3 * DIM, DIM), jnp.float32) * 0.02
        qkv_b = jnp.zeros((3 * DIM,), jnp.float32)
        rpb = jax.random.normal(ks[2], (HEADS, 2 * K - 1), jnp.float32) * 0.02
        proj_w = jax.random.normal(ks[3], (DIM, DIM), jnp.float32) * 0.02
        proj_b = jnp.zeros((DIM,), jnp.float32)
        return dict(x=x, qkv_w=qkv_w, qkv_b=qkv_b, rpb=rpb, proj_w=proj_w, proj_b=proj_b)
    _L0_attn_all = _L0_attn_setup()
    _L0_attn_in = {k: v for k, v in _L0_attn_all.items() if k in ('qkv_w', 'qkv_b', 'rpb', 'proj_w', 'proj_b')}
    del _L0_attn_all

    def _L0_ffn_setup():
        import jax, jax.numpy as jnp
        import numpy as np
        DM = 256
        NEXPERTS = 32
        EXPERTSETS = 4
        EXPERTSIZE = 32
        BATCH, SEQ = (4, 512)
        key = jax.random.key(seed)
        k0, k1, k2, k3 = jax.random.split(key, 4)
        scale = 0.02
        x = jax.random.normal(k0, (BATCH, SEQ, DM), jnp.float32)
        controller = jax.random.normal(k1, (DM, NEXPERTS, EXPERTSETS), jnp.float32) * scale
        f1 = jax.random.normal(k2, (DM, NEXPERTS, EXPERTSETS, EXPERTSIZE), jnp.float32) * scale
        bias = jnp.zeros((NEXPERTS, EXPERTSETS, EXPERTSIZE), jnp.float32)
        f2 = jax.random.normal(k3, (NEXPERTS, EXPERTSETS, EXPERTSIZE, DM), jnp.float32) * scale
        return {'x': x, 'controller': controller, 'f1': f1, 'bias': bias, 'f2': f2}
    _L0_ffn_all = _L0_ffn_setup()
    _L0_ffn_in = {k: v for k, v in _L0_ffn_all.items() if k in ('controller', 'f1', 'bias', 'f2')}
    del _L0_ffn_all
    return {'x': x, 'L0_tok_weight': _L0_tok_in['weight'], 'L0_tok_weighted_sum': _L0_tok_in['weighted_sum'], 'L0_attn_qkv_w': _L0_attn_in['qkv_w'], 'L0_attn_qkv_b': _L0_attn_in['qkv_b'], 'L0_attn_rpb': _L0_attn_in['rpb'], 'L0_attn_proj_w': _L0_attn_in['proj_w'], 'L0_attn_proj_b': _L0_attn_in['proj_b'], 'L0_ffn_controller': _L0_ffn_in['controller'], 'L0_ffn_f1': _L0_ffn_in['f1'], 'L0_ffn_bias': _L0_ffn_in['bias'], 'L0_ffn_f2': _L0_ffn_in['f2']}

def reference(x, L0_tok_weight, L0_tok_weighted_sum, L0_attn_qkv_w, L0_attn_qkv_b, L0_attn_rpb, L0_attn_proj_w, L0_attn_proj_b, L0_ffn_controller, L0_ffn_f1, L0_ffn_bias, L0_ffn_f2):
    import jax
    import jax.numpy as jnp

    def _L0_tok_ref(x, weight, weighted_sum):
        import jax, jax.numpy as jnp
        import numpy as np
        return jnp.einsum('bhid,oi,od->bho', x, weighted_sum, weight)

    def _L0_attn_ref(x, qkv_w, qkv_b, rpb, proj_w, proj_b):
        import jax, jax.numpy as jnp
        import numpy as np
        DIM = 256
        HEADS = 16
        HEAD_DIM = DIM // HEADS
        K = 13
        NS = K // 2
        SCALE = HEAD_DIM ** (-0.5)
        B, L, C = x.shape
        qkv = (x @ qkv_w.T + qkv_b).reshape(B, L, 3, HEADS, HEAD_DIM).transpose(2, 0, 3, 1, 4)
        q, k, v = (qkv[0] * SCALE, qkv[1], qkv[2])
        i = jnp.arange(L)
        ni = jnp.clip(i - NS, 0, L - K)
        pi = NS + jnp.where(i < NS, NS - i, 0) + jnp.where(i + NS >= L, L - i - 1 - NS, 0)
        j = jnp.arange(K)
        nbr = ni[:, None] + j[None, :]
        bidx = pi[:, None] + j[None, :]
        kg = k[:, :, nbr, :]
        vg = v[:, :, nbr, :]
        attn = jnp.einsum('bhld,bhlkd->bhlk', q, kg) + rpb[:, bidx][None]
        attn = jax.nn.softmax(attn, axis=-1)
        out = jnp.einsum('bhlk,bhlkd->bhld', attn, vg)
        out = out.transpose(0, 2, 1, 3).reshape(B, L, C)
        return out @ proj_w.T + proj_b

    def _L0_ffn_ref(x, controller, f1, bias, f2):
        import jax, jax.numpy as jnp
        import numpy as np
        DM = 256
        NEXPERTS = 32
        EXPERTSETS = 4
        EXPERTSIZE = 32
        BATCH, SEQ = (4, 512)
        B, L, d = x.shape
        t = controller.shape[1]
        g = L // t
        grouped = x.reshape(B, g, t, d)
        logits = jnp.einsum('bgtd,des->bgtes', grouped, controller)
        tie = jnp.linspace(0.0, 1e-06, t, dtype=logits.dtype).reshape(t, 1, 1)
        logits = logits + tie
        perm = (logits == jnp.max(logits, axis=-3, keepdims=True)).astype(x.dtype)
        perm = jax.lax.stop_gradient(perm)
        dispatched = jnp.einsum('bgtd,bgtes->bgesd', grouped, perm)
        inner = jax.nn.relu(jnp.einsum('bgesd,desf->bgesf', dispatched, f1) + bias)
        intermediate = jnp.einsum('bgesf,esfd->bgesd', inner, f2)
        out = jnp.einsum('bgesd,bgtes->bgtd', intermediate, perm)
        return out.reshape(B, L, d)
    h = _L0_tok_ref(x, L0_tok_weight, L0_tok_weighted_sum)
    h = h + _L0_attn_ref(_layernorm(h, axis=-1), L0_attn_qkv_w, L0_attn_qkv_b, L0_attn_rpb, L0_attn_proj_w, L0_attn_proj_b)
    h = h + _L0_ffn_ref(_layernorm(h, axis=-1), L0_ffn_controller, L0_ffn_f1, L0_ffn_bias, L0_ffn_f2)
    return h

_drawn_inputs = setup_inputs


def setup_inputs(seed=0):
    import zlib

    import numpy as np

    out = dict(_drawn_inputs(seed))
    spreads = {'L0_attn_qkv_b': (0.0, 0.1), 'L0_attn_proj_b': (0.0, 0.1), 'L0_ffn_bias': (0.0, 0.1)}
    factors = {'L0_attn_rpb': 7.167}
    for name, (base, spread) in spreads.items():
        noise = np.random.default_rng([zlib.crc32(name.encode()), seed]).standard_normal(out[name].shape)
        drawn = base * np.exp(spread * noise) if base else spread * noise
        out[name] = jnp.asarray(drawn.astype(out[name].dtype))
    for name, factor in factors.items():
        out[name] = (out[name] * factor).astype(out[name].dtype)
    return out
```

```python
from contextlib import ExitStack

import numpy as np

import concourse.bass as bass
from concourse import mybir

F32 = mybir.dt.float32
ALU = mybir.AluOpType
ACT = mybir.ActivationFunctionType
AX = mybir.AxisListType

P = 128
BATCH, SEQ, C, TAPS = 4, 512, 256, 4
TILES = SEQ // P
NT = BATCH * TILES
KIN = C * TAPS
HEADS, HD, WIN = 16, 16, 13
RPB = 2 * WIN - 1
BLK = 16
KEYS = 32
NBLK = SEQ // BLK
MASKED = -1.0e38
EPS = 1e-5
GROUP = 32
NG = BATCH * SEQ // GROUP
EXPERTS, FF = 128, 32
ROUND = 8

PREP = (5, 4)


def key_base(blk):
    return min(max(BLK * blk - 8, 0), SEQ - KEYS)


def neighbourhood(blk, q):
    query = BLK * blk + q
    first = min(max(query - WIN // 2, 0), SEQ - WIN)
    return first - key_base(blk), first - query + WIN - 1


def build(nc, x, w_taps, w_sum, qkv_w, qkv_b, rpb, proj_w, proj_b, controller, f1, f_bias, f2, ties, out):
    x_d = x.rearrange("b (t p) i d -> (b t) p (i d)", p=P)
    out_d = out.rearrange("b (t p) c -> (b t) p c", p=P)
    f1_d = f1.rearrange("(k p) e s f -> p k (e s f)", p=P)
    f2_d = f2.rearrange("e s f d -> (e s f) d")
    v_scratch = nc.dram_tensor("v_scratch", [SEQ, C], F32, kind="Internal").ap()

    with ExitStack() as ctx:
        ctx.enter_context(nc.allow_non_contiguous_dma(reason="small weights and windows"))

        def sb(name, *shape):
            return ctx.enter_context(nc.sbuf_tensor(name, [P, *shape], F32))

        def sem(name):
            return ctx.enter_context(nc.semaphore(name))

        bank = [ctx.enter_context(nc.psum_tensor(f"bank{i}", [P, 512], F32)) for i in range(8)]

        ident = sb("ident", P)
        parity = sb("parity", 2)
        quarter = sb("quarter", 4)
        h = sb("h", NT, C)
        xn2 = sb("xn2", NT, C)
        permT = sb("permT", NT * P)
        f_biasT = sb("f_biasT", 32)

        ARENA = 41 * 1024
        arena = sb("arena", ARENA)
        top = [0, 0]

        def carve(phase, *shape):
            n = int(np.prod(shape))
            ap = arena[:, top[phase]:top[phase] + n]
            top[phase] += n
            assert top[phase] <= ARENA, (phase, top)
            names = "abcde"[:len(shape)]
            return ap.rearrange(f"p ({' '.join(names)}) -> p {' '.join(names)}",
                                **dict(zip(names, shape))) if len(shape) > 1 else ap

        x_sb = carve(0, TILES, KIN)
        h1, hb, h2 = (carve(0, TILES, C) for _ in range(3))
        xT = carve(0, 2, 8, P)
        w_tok = carve(0, 8, C)
        w_qkv = carve(0, 2, 3 * C)
        w_proj = carve(0, 2, C)
        ctl = carve(0, 2, EXPERTS)
        xn = carve(0, TILES, C)
        xnT = carve(0, 2, SEQ)
        q_eo = carve(0, 2, NBLK, 2, BLK)
        kT = carve(0, 2, SEQ)
        k_bd = carve(0, 2, 4, SEQ)
        v_sb = carve(0, TILES, C)
        v_bd = carve(0, NBLK, 4, 2, 32)
        score = carve(0, TILES, 4, P)
        probT = carve(0, 2, 4, P)
        even = carve(0, 2, 256)
        att = carve(0, TILES, 2, P)
        attT = carve(0, 2, 2, P)
        xn2c, xn2T = xn, xnT
        logit = carve(0, SEQ)
        bias_tab = carve(0, 4, 256)
        v_bias = carve(0, C)
        p_bias = carve(0, C)
        tie = carve(0, GROUP)
        row_max = carve(0, TILES, 16)
        row_sum = carve(0, TILES, 16)
        row_inv = carve(0, TILES, 16)
        stat = carve(0, TILES, 6)
        mean_var = carve(0, TILES, 2)
        var_eps = carve(0, TILES)
        rstd = carve(0, TILES)
        minus_half = carve(0, TILES)
        stat2 = carve(0, TILES, 6)
        mean_var2 = carve(0, TILES, 2)
        var_eps2 = carve(0, TILES)
        rstd2 = carve(0, TILES)
        qkv_bc = carve(0, 4)
        q_scale = carve(0, 2)
        q_bias = carve(0, 2, 2)
        gmax = carve(0, SEQ // GROUP)
        w_sum_sb = k_bd[:, 0, 0:1, :].rearrange("p a (o i) -> p (a o) i", o=2)
        w_taps_sb = k_bd[:, 0, 1, 0:8].rearrange("p (o d) -> p o d", o=2)
        w_mix = v_bd[:, 0:8, :, :, :].rearrange("p a b c d -> p (a b c d)").rearrange(
            "p (o i d) -> p o i d", o=2, d=TAPS)
        qkv_sb = v_bd[:, 8:14, :, :, :].rearrange("p a b c d -> p a (b c d)")
        proj_sb = v_bd[:, 14:16, :, :, :].rearrange("p a b c d -> p a (b c d)")
        f_bias_sb = v_bd[0:32, 16, :, :, :].rearrange("p b c d -> p (b c d)")[:, 0:P]
        tab_sb = v_bd[0:32, 17:20, :, :, :].rearrange("p v b c d -> p v (b c d)")

        dispT = carve(1, 2, EXPERTS, NG)
        inter = dispT.rearrange("p a e g -> p (a e g)").rearrange("p (g c) -> p g c", c=C)
        f1_ring = carve(1, 2, 2, 4, ROUND * FF)
        f2_sb = carve(1, 32, C)
        innerT = carve(1, 32, NG)
        inner_bd = carve(1, 2, 4, 2, P)
        stage = carve(1, 8, 2, C)
        x_cur = carve(1, 2, C)
        perm_cur = carve(1, 2, P)
        perm_bd = carve(1, 2, 4, P)
        y_sb = carve(1, 4, C)

        filled = [sem(f"filled{i}") for i in range(8)]
        copied = [sem(f"copied{i}") for i in range(8)]
        x_loaded = [sem(f"x_loaded{i}") for i in range(TILES)]
        ident_zero, ident_ready, masks_ready = sem("ident_zero"), sem("ident_ready"), sem("masks_ready")
        tok_w_loaded, qkv_w_loaded, vec_loaded = sem("tok_w_loaded"), sem("qkv_w_loaded"), sem("vec_loaded")
        w_mixed, q_consts = sem("w_mixed"), sem("q_consts")
        tab_masked, tab_loaded, tab_spread = sem("tab_masked"), sem("tab_loaded"), sem("tab_spread")
        bd_zeroed, half_set = sem("bd_zeroed"), sem("half_set")
        stat_done, aggr_done, eps_added, rstd_ready = (sem(n) for n in ("stat_done", "aggr_done", "eps_added", "rstd_ready"))
        xn_ready, hb_ready = sem("xn_ready"), sem("hb_ready")
        k_spread, v_written, v_spread = sem("k_spread"), sem("v_written"), sem("v_spread")
        max_done, shifted, exp_done, sum_done, inv_done = (sem(n) for n in ("max_done", "shifted", "exp_done", "sum_done", "inv_done"))
        even_done, att_scaled = sem("even_done"), sem("att_scaled")
        h2_done, stat2_done, aggr2_done, eps2_added, rstd2_ready = (sem(n) for n in ("h2_done", "stat2_done", "aggr2_done", "eps2_added", "rstd2_ready"))
        xn2_ready, xn2_kept = sem("xn2_ready"), sem("xn2_kept")
        gmax_done, perm_done = sem("gmax_done"), sem("perm_done")
        cur_ready = sem("cur_ready")
        f1_loaded = [sem(f"f1_loaded{i}") for i in range(2)]
        f2_loaded = sem("f2_loaded")
        inner_zeroed, inner_spread_a, inner_spread_v = sem("inner_zeroed"), sem("inner_spread_a"), sem("inner_spread_v")
        moved = [sem(f"moved{i}") for i in range(8)]
        comb_ready = sem("comb_ready")
        y_stored = [sem(f"y_stored{i}") for i in range(4)]

        block = ctx.enter_context(nc.Block())

        def jobs_in(b):
            return 5 + 8 * b, 4 + 9 * b, 4 + 8 * b, 2 + 3 * b
        END01, END2, END3, ENDW = 32, 36, 32, 12

        MIX0 = [PREP[0] + END01 + 8, PREP[1] + END01 + 8, END2, END3] + [ENDW + 8 + 2, ENDW + 8 + 2, ENDW + 8, ENDW + 8]
        COMB0 = [END2 + 4, END3 + 4]

        @block.sync
        def _(sp):
            def load_x(b, waits):
                for t in range(TILES):
                    if waits is not None:
                        sp.wait_ge(copied[1], waits + t + 1)
                    sp.dma_start(x_sb[:, t, :], x_d[4 * b + t, :, :] if isinstance(b, int) else
                                 x_d[bass.ds(4 * b + t, 1), :, :].rearrange("a p n -> (a p) n")).then_inc(x_loaded[t], 16)

            def spread_kv(b, jw, j2, j3, first):
                for i in (6, 7):
                    sp.wait_ge(copied[i], jw + 1)
                for g in range(4):
                    sp.dma_start(k_bd[32 * g:32 * g + 32, :, g, :], kT[32 * g:32 * g + 32, :, :]).then_inc(k_spread, 16)
                sp.wait_ge(copied[2], j2)
                sp.wait_ge(copied[3], j3)
                if not first:
                    sp.wait_ge(v_spread, 128 * b)
                sp.dma_start(v_scratch.rearrange("(t p) c -> p t c", p=P), v_sb[:, :, :]).then_inc(v_written, 16)
                sp.wait_ge(v_written, 16 * (b + 1))
                for g in range(4):
                    rows = slice(32 * g, 32 * g + 32)
                    inner = bass.AP(v_scratch.tensor, (BLK - 8) * C + 64 * g, [[C, KEYS], [BLK * C, NBLK - 2], [1, 64]])
                    edges = bass.AP(v_scratch.tensor, 64 * g, [[C, KEYS], [(SEQ - KEYS) * C, 2], [1, 64]])
                    v4 = v_bd[rows, :, g, :, :].rearrange("p n a c -> p n (a c)")
                    sp.dma_start(v4[:, 1:NBLK - 1, :], inner).then_inc(v_spread, 16)
                    sp.dma_start(v4[:, 0:NBLK:NBLK - 1, :], edges).then_inc(v_spread, 16)

            sp.dma_start(w_sum_sb, w_sum.rearrange("(o p) i -> p o i", p=P)).then_inc(tok_w_loaded, 16)
            sp.dma_start(w_taps_sb, w_taps.rearrange("(o p) d -> p o d", p=P)).then_inc(tok_w_loaded, 16)
            load_x(0, None)
            sp.dma_start(qkv_sb, qkv_w.rearrange("(r p) c -> p r c", p=P)).then_inc(qkv_w_loaded, 16)
            for r in range(2):
                for a in range(2):
                    sp.dma_start(proj_sb[:, r, a * P:(a + 1) * P].rearrange("p (n d) -> p n d", d=HD),
                                 proj_w[r * P:(r + 1) * P, :].rearrange("p (n a d) -> p a n d", a=2, d=HD)[:, a, :, :]).then_inc(qkv_w_loaded, 16)
            sp.dma_start(f_bias_sb.rearrange("g (j f) -> g j f", j=4),
                         f_bias.rearrange("e s f -> (e s f)").rearrange("(j g f) -> g j f", j=4, g=32)).then_inc(qkv_w_loaded, 16)
            sp.dma_start(ctl, controller.rearrange("(k p) e s -> p k (e s)", p=P)).then_inc(vec_loaded, 16)
            sp.dma_start(qkv_bc, qkv_b.rearrange("(r p) -> p r", p=P)[:, 0:4]).then_inc(vec_loaded, 16)
            for a in range(2):
                sp.dma_start(v_bias.rearrange("p (g a c) -> p a g c", g=4, a=2)[:, a, :, :],
                             bass.AP(qkv_b.tensor, 2 * C + 128 * a, [[0, P], [32, 4], [1, 32]])).then_inc(vec_loaded, 16)
            sp.dma_start(p_bias, bass.AP(proj_b.tensor, 0, [[0, P], [1, C]])).then_inc(vec_loaded, 16)
            sp.dma_start(tie, bass.AP(ties.tensor, 0, [[0, P], [1, GROUP]])).then_inc(vec_loaded, 16)
            sp.wait_ge(tab_masked, 1)
            for v, blk in enumerate((0, 1, NBLK - 1)):
                for q in range(BLK):
                    r0, s0 = neighbourhood(blk, q)
                    for par in range(2):
                        sp.dma_start(tab_sb[16 * par + q:16 * par + q + 1, v, :].rearrange("p (n r) -> p n r", r=KEYS)[:, :, r0:r0 + WIN],
                                     bass.AP(rpb.tensor, par * RPB + s0, [[0, 1], [2 * RPB, 8], [1, WIN]])).then_inc(tab_loaded, 16)
            sp.wait_ge(tab_loaded, 16 * 96)
            for quad in range(4):
                for c in range(4):
                    v = 0 if (quad, c) == (0, 0) else 2 if (quad, c) == (3, 3) else 1
                    sp.dma_start(bias_tab[32 * c:32 * c + 32, quad, :], tab_sb[:, v, :]).then_inc(tab_spread, 16)
            sp.wait_ge(tab_spread, 256)
            sp.wait_ge(bd_zeroed, 1)
            spread_kv(0, 0, 4, 4, True)
            load_x(1, PREP[1])
            with sp.Fori(0, 2) as b:
                j01, j2, j3, jw = jobs_in(b)
                spread_kv(b + 1, jw + 1, j2 + 8, j3 + 8, False)
                load_x(b + 2, PREP[1] + j01)
            j01, j2, j3, jw = jobs_in(2)
            spread_kv(3, jw + 1, j2 + 8, j3 + 8, False)
            sp.wait_ge(perm_done, BATCH)
            sp.wait_ge(h2_done, BATCH)
            def load_f1(s, rnd):
                for k in range(2):
                    sp.dma_start(f1_ring[:, s, k, :, :],
                                 f1_d.rearrange("p k (j g n) -> p k j g n", j=4, g=4)[:, k, :, rnd, :]).then_inc(f1_loaded[s], 16)
            for s in range(2):
                load_f1(s, s)
            for j in range(4):
                sp.dma_start(f2_sb[32 * j:32 * j + 32, :, :],
                             f2_d.rearrange("(j g f) d -> j f g d", j=4, g=32)[j]).then_inc(f2_loaded, 16)
            for s in range(2):
                sp.wait_ge(filled[4 + s], ENDW + 8 + 1)
                load_f1(s, 2 + s)
            for u in range(ROUND):
                for i in range(4):
                    s = 4 * (u % 2) + i
                    sp.wait_ge(copied[s], MIX0[s] + u // 2 + 1)
                    if u == 0 and i == 0:
                        for bk in (4, 5):
                            sp.wait_ge(filled[bk], ENDW + 8 + 2)
                    g = 8 * i + u
                    for j in range(4):
                        sp.dma_start(inter[32 * j + g:32 * j + g + 1, :, :].rearrange("p (l a) c -> p l (a c)", a=2),
                                     stage[32 * j:32 * j + 32, s, :, :].rearrange("l a c -> l (a c)")).then_inc(moved[s], 16)
            for t in range(NT):
                sp.wait_ge(copied[2 + t % 2], COMB0[t % 2] + t // 2 + 1)
                sp.dma_start(out_d[t], y_sb[:, t % 4, :]).then_inc(y_stored[t % 4], 16)
            for s in range(4):
                sp.wait_ge(y_stored[s], 16 * (NT // 4))

        @block.tensor
        def _(pe):
            def room(i, job):
                if not (isinstance(job, int) and job == 0):
                    pe.wait_ge(copied[i], job)

            def turn4(i, job, sources):
                room(i, job)
                n = 0
                for s in sources:
                    k, m = s.shape[0], int(np.prod(s.shape[1:]))
                    last = nc.tensor.transpose(bank[i][0:m, n:n + k], s, ident[0:k, 0:k])
                    n += k
                last.then_inc(filled[i], 1)

            def weights():
                pe.wait_ge(ident_ready, 1)
                pe.wait_ge(w_mixed, 2)
                for n in range(4):
                    turn4(n % 2, n // 2, [w_mix.rearrange("p o i d -> p o (i d)")[:, o, k * P:(k + 1) * P]
                                          for k in (2 * n, 2 * n + 1) for o in range(2)])
                pe.wait_ge(qkv_w_loaded, 96)
                for n in range(3):
                    turn4(n % 2, 2 + n // 2, [qkv_sb[:, r, k * P:(k + 1) * P] for r in (2 * n, 2 * n + 1) for k in range(2)])
                turn4(1, 3, [proj_sb[:, o, a * P:(a + 1) * P] for a in range(2) for o in range(2)])
                turn4(0, 4, [f_bias_sb])

            def token_products(t, j2, j3, j01):
                i, j = (2, j2) if t % 2 == 0 else (3, j3)
                pe.wait_ge(copied[0], PREP[0] + j01 + t + 1)
                pe.wait_ge(copied[1], PREP[1] + j01 + t + 1)
                room(i, j + t // 2)
                for k in range(8):
                    last = nc.tensor.matmul(bank[i][:, 0:C], xT[:, t % 2, k, :], w_tok[:, k, :], start=(k == 0), stop=(k == 7))
                last.then_inc(filled[i], 1)

            def tokens(b, j01, j2, j3):
                for t in range(TILES):
                    pe.wait_ge(x_loaded[t], 16 * (b + 1))
                    for i in range(2):
                        turn4(i, PREP[i] + j01 + t, [x_sb[:, t, (4 * i + k) * P:(4 * i + k + 1) * P] for k in range(4)])
                    if t:
                        token_products(t - 1, j2, j3, j01)
                token_products(TILES - 1, j2, j3, j01)

            def project(b, j01, j2, j3, jw):
                pe.wait_ge(xn_ready, 4 * (b + 1))
                for i in range(2):
                    turn4(i, PREP[i] + j01, [xn[:, t, i * P:(i + 1) * P] for t in range(TILES)])
                for i in range(2):
                    pe.wait_ge(copied[i], PREP[i] + j01 + 1)
                for r in (2, 3, 0, 1):
                    room(4 + r, jw)
                    for k in range(2):
                        last = nc.tensor.matmul(bank[4 + r][:, :], w_qkv[:, k, r * P:(r + 1) * P], xnT[:, k, :], start=(k == 0), stop=(k == 1))
                    last.then_inc(filled[4 + r], 1)
                for t in range(TILES):
                    i, j = (2, j2) if t % 2 == 0 else (3, j3)
                    room(i, j + t // 2)
                    for k in range(2):
                        last = nc.tensor.matmul(bank[i][:, 0:C], xnT[:, k, t * P:(t + 1) * P], w_qkv[:, k, 2 * C:3 * C], start=(k == 0), stop=(k == 1))
                    last.then_inc(filled[i], 1)

            def scores(b, jw):
                pe.wait_ge(k_spread, 64 * (b + 1))
                for i in (4, 5):
                    pe.wait_ge(copied[i], jw)
                for t in range(TILES):
                    room(4 + t, jw)
                    for n in range(4):
                        for c in range(4):
                            blk, half = 8 * t + 4 * (n // 2) + c, n % 2
                            last = nc.tensor.matmul(bank[4 + t][32 * c:32 * c + 32, n * P:(n + 1) * P],
                                                    q_eo[:, half, blk, :, :].rearrange("p a q -> p (a q)"),
                                                    k_bd[:, half, :, key_base(blk):key_base(blk) + KEYS],
                                                    start=True, stop=True, tile_position=(0, 32 * c))
                    last.then_inc(filled[4 + t], 1)

            def attend(b, j01, j2, j3, jw):
                def turn_probs(t):
                    pe.wait_ge(exp_done, 4 * b + t + 1)
                    turn4(t % 2, PREP[t % 2] + j01 + t // 2, [score[:, t, n, :] for n in range(4)])

                def values(t):
                    pe.wait_ge(copied[t % 2], PREP[t % 2] + j01 + t // 2 + 1)
                    room(4 + t, jw)
                    for n in range(4):
                        for c in range(4):
                            blk, half = 8 * t + 4 * (n // 2) + c, n % 2
                            last = nc.tensor.matmul(bank[4 + t][32 * c:32 * c + 32, n * P:(n + 1) * P],
                                                    probT[:, t % 2, n, 32 * c:32 * c + 32],
                                                    v_bd[:, blk, :, half, :],
                                                    start=True, stop=True, tile_position=(0, 32 * c))
                    last.then_inc(filled[4 + t], 1)

                def turn_att(t):
                    pe.wait_ge(att_scaled, 4 * b + t + 1)
                    turn4(2, j2 + t, [att[:, t, n, :] for n in range(2)])

                def out_proj(t):
                    pe.wait_ge(copied[2], j2 + t + 1)
                    room(3, j3 + t)
                    for a in range(2):
                        last = nc.tensor.matmul(bank[3][:, 0:C], attT[:, t % 2, a, :], w_proj[:, a, :], start=(a == 0), stop=(a == 1))
                    last.then_inc(filled[3], 1)

                turn_probs(0)
                turn_probs(1)
                pe.wait_ge(v_spread, 128 * (b + 1))
                values(0)
                turn_probs(2)
                values(1)
                turn_att(0)
                turn_probs(3)
                values(2)
                turn_att(1)
                out_proj(0)
                values(3)
                turn_att(2)
                out_proj(1)
                turn_att(3)
                out_proj(2)
                out_proj(3)

            def route(b, j01, j2):
                pe.wait_ge(xn2_ready, 4 * (b + 1))
                for i in range(2):
                    turn4(i, PREP[i] + j01, [xn2c[:, t, i * P:(i + 1) * P] for t in range(TILES)])
                for i in range(2):
                    pe.wait_ge(copied[i], PREP[i] + j01 + 1)
                room(2, j2)
                for k in range(2):
                    last = nc.tensor.matmul(bank[2][:, :], ctl[:, k, :], xn2T[:, k, :], start=(k == 0), stop=(k == 1))
                last.then_inc(filled[2], 1)

            weights()
            pe.wait_ge(copied[0], PREP[0])
            pe.wait_ge(copied[1], PREP[1])
            pe.wait_ge(vec_loaded, 96)
            tokens(0, 0, 0, 0)
            project(0, 4, 2, 2, 0)
            scores(0, 1)
            with pe.Fori(0, 3) as b:
                j01, j2, j3, jw = jobs_in(b)
                tokens(b + 1, j01, j2, j3)
                attend(b, j01 + 4, j2 + 2, j3 + 2, jw)
                project(b + 1, j01 + 6, j2 + 6, j3 + 6, jw + 1)
                route(b, j01 + 7, j2 + 8)
                scores(b + 1, jw + 2)
            attend(3, 29, 31, 28, 11)
            route(3, 31, 35)

            with pe.Fori(0, NT // 2) as i2:
                for s in range(2):
                    pe.wait_ge(cur_ready, 4 * i2 + 2 * s + 2)
                    turn4(s, PREP[s] + END01 + i2, [perm_cur[:, s, :]])
                for s in range(2):
                    pe.wait_ge(copied[s], PREP[s] + END01 + i2 + 1)
                    for half in range(2):
                        k = 4 + 2 * s + half
                        room(k, ENDW + i2)
                        nc.tensor.matmul(bank[k][:, :], x_cur[:, s, half * P:(half + 1) * P], perm_bd[:, s, :, :],
                                         start=True, stop=True).then_inc(filled[k], 1)
            for k in range(4, 8):
                pe.wait_ge(copied[k], ENDW + 8)
            for rnd in range(4):
                s = rnd % 2
                pe.wait_ge(f1_loaded[s], 32 * (rnd // 2 + 1))
                room(4 + s, ENDW + 8 + rnd // 2)
                for g in range(ROUND):
                    for k in range(2):
                        for j in range(4):
                            last = nc.tensor.matmul(bank[4 + s][32 * j:32 * j + 32, g * NG:(g + 1) * NG],
                                                    f1_ring[:, s, k, j, g * FF:(g + 1) * FF],
                                                    dispT[:, k, 32 * j + 8 * rnd + g, :],
                                                    start=(k == 0), stop=(k == 1), tile_position=(0, 32 * j))
                last.then_inc(filled[4 + s], 1)
            pe.wait_ge(f2_loaded, 64)
            for u in range(ROUND):
                pe.wait_ge(inner_spread_a, 2 * (u + 1))
                pe.wait_ge(inner_spread_v, 2 * (u + 1))
                for i in range(4):
                    s = 4 * (u % 2) + i
                    room(s, MIX0[s] + u // 2)
                    for a in range(2):
                        last = nc.tensor.matmul(bank[s][:, a * C:(a + 1) * C], inner_bd[:, u % 2, i, a, :],
                                                f2_sb[:, 8 * i + u, :], start=True, stop=True)
                    last.then_inc(filled[s], 1)
            for s in range(8):
                pe.wait_ge(moved[s], 16 * 16)
            for t in range(NT):
                pe.wait_ge(comb_ready, t + 1)
                room(2 + t % 2, COMB0[t % 2] + t // 2)
                for c in range(4):
                    last = nc.tensor.matmul(bank[2 + t % 2][32 * c:32 * c + 32, 0:C], perm_cur[:, t % 2, 32 * c:32 * c + 32],
                                            inter[:, 4 * t + c, :], start=True, stop=True, tile_position=(0, 32 * c))
                last.then_inc(filled[2 + t % 2], 1)

        def weights_qkv(eng, copy, i, ns):
            for n in ns:
                eng.wait_ge(filled[i], 3 + n // 2)
                src = bank[i].rearrange("p (r k o) -> p r k o", r=2, k=2)
                if n < 2:
                    dst = w_qkv[:, :, 2 * n * P:(2 * n + 2) * P].rearrange("p k (r o) -> p r k o", r=2)
                    for r in range(2):
                        last = copy(dst[:, r, :, :], src[:, r, :, :])
                else:
                    dst = w_qkv[:, :, 2 * C:3 * C].rearrange("p k (g a c) -> p a k g c", g=4, a=2)
                    for r in range(2):
                        last = copy(dst[:, r, :, :, :], src[:, r, :, :].rearrange("p k (g c) -> p k g c", g=4))
                last.then_inc(copied[i], 1)

        def spread_inner(eng, u, js, done):
            if u == 0:
                for k in (4, 5):
                    eng.wait_ge(copied[k], ENDW + 8 + 2)
                eng.wait_ge(inner_zeroed, 1)
            if u >= 2:
                for s in range(4 * (u % 2), 4 * (u % 2) + 4):
                    eng.wait_ge(filled[s], MIX0[s] + (u - 2) // 2 + 1)
            for j in js:
                rows = slice(32 * j, 32 * j + 32)
                dst = inner_bd[rows, u % 2, :, :, 32 * j:32 * j + 32]
                src = innerT[rows, u:32:ROUND, :].rearrange("p i (l a) -> p i a l", a=2)
                if done is inner_spread_a:
                    nc.scalar.activation(dst, src, ACT.Relu).then_inc(done, 1)
                else:
                    nc.vector.tensor_scalar(dst, src, 0.0, None, ALU.max).then_inc(done, 1)

        def take_mixed(eng, copy, u, i):
            s = 4 * (u % 2) + i
            job = MIX0[s] + u // 2
            eng.wait_ge(filled[s], job + 1)
            if u >= 2:
                eng.wait_ge(moved[s], 64 * (u // 2))
            copy(stage[:, s, :, :].rearrange("p a c -> p (a c)"), bank[s][:, :]).then_inc(copied[s], 1)

        @block.scalar
        def _(act):
            def take(i, job, dst, src):
                act.wait_ge(filled[i], job + 1)
                nc.scalar.copy(dst, src).then_inc(copied[i], 1)

            def tokens(j01, j2, j3):
                for t in range(TILES):
                    if t >= 2:
                        act.wait_ge(filled[2 + t % 2], (j2, j3)[t % 2] + 1)
                    take(0, PREP[0] + j01 + t, xT[:, t % 2, 0:4, :].rearrange("p k m -> p (k m)"), bank[0][:, :])
                    yield t

            def exps(b, t):
                act.wait_ge(shifted, 4 * b + t + 1)
                nc.scalar.activation(score[:, t, :, :], score[:, t, :, :], ACT.Exp).then_inc(exp_done, 1)

            def project(j01, jw):
                take(0, PREP[0] + j01, xnT[:, 0, :], bank[0][:, :])
                for half in range(2):
                    act.wait_ge(filled[4 + half], jw + 1)
                    for a in range(2):
                        last = nc.scalar.activation(q_eo[:, half, :, a, :], bank[4 + half].rearrange("p (n q) -> p n q", q=BLK), ACT.Identity,
                                                    bias=q_bias[:, half, a:a + 1], scale=q_scale[:, a:a + 1])
                    last.then_inc(copied[4 + half], 1)

            def attend(b, j01, jw):
                def probs(t):
                    if t >= 2:
                        act.wait_ge(filled[4 + t - 2], jw + 1)
                    take(0, PREP[0] + j01 + t // 2, probT[:, t % 2, :, :].rearrange("p n m -> p (n m)"), bank[0][:, :])

                def evens(t):
                    act.wait_ge(filled[4 + t], jw + 1)
                    if t >= 2:
                        act.wait_ge(copied[4 + t - 2], jw + 1)
                    nc.scalar.mul(even[:, t % 2, :].rearrange("p (n d) -> p n d", d=HD),
                                  bank[4 + t].rearrange("p (n a d) -> p n a d", a=2, d=HD)[:, :, 0, :],
                                  parity[:, 0:1]).then_inc(even_done, 1)
                probs(0)
                evens(0)
                probs(2)
                evens(1)
                evens(2)
                evens(3)

            def route(j01):
                take(0, PREP[0] + j01, xn2T[:, 0, :], bank[0][:, :])

            for n in (0, 2):
                take(0, n // 2, w_tok[:, 2 * n:2 * n + 2, :].rearrange("p k o -> p (k o)"), bank[0][:, :])
            weights_qkv(act, nc.scalar.copy, 0, (0, 2))
            take(0, 4, f_biasT[:, :], bank[0][:, 0:32])
            for t in tokens(0, 0, 0):
                pass
            act.wait_ge(q_consts, 3)
            project(4, 0)
            with act.Fori(0, 3) as b:
                j01, j2, j3, jw = jobs_in(b)
                for t in tokens(j01, j2, j3):
                    exps(b, t)
                attend(b, j01 + 4, jw)
                project(j01 + 6, jw + 1)
                route(j01 + 7)
            for t in range(TILES):
                exps(3, t)
            attend(3, 29, 11)
            route(31)
            act.wait_ge(perm_done, BATCH)
            with act.Fori(0, NT // 2) as i2:
                for s in range(2):
                    k = 4 + 2 * s
                    act.wait_ge(filled[k], ENDW + i2 + 1)
                    nc.scalar.copy(dispT[:, 0, :, bass.ds(8 * i2 + 4 * s, 4)],
                                   bank[k].rearrange("p (c e) -> p e c", c=4)).then_inc(copied[k], 1)
            for u in range(ROUND):
                spread_inner(act, u, (0, 1), inner_spread_a)
                for i in (0, 2):
                    take_mixed(act, nc.scalar.copy, u, i)

        @block.vector
        def _(dve):
            def take(i, job, dst, src):
                dve.wait_ge(filled[i], job + 1)
                nc.vector.tensor_copy(dst, src).then_inc(copied[i], 1)

            def tile_of(tensor, n):
                return tensor[:, bass.ds(n, 1), :].rearrange("p a c -> p (a c)")

            def keep_h(b, t, j2, j3):
                i, j = (2, j2) if t % 2 == 0 else (3, j3)
                if t == 0 and not (isinstance(b, int) and b == 0):
                    dve.wait_ge(hb_ready, 4 * b)
                dve.wait_ge(filled[i], j + t // 2 + 1)
                nc.vector.bn_stats(stat[:, t, :], bank[i][:, 0:C]).then_inc(stat_done, 1)
                nc.vector.tensor_copy(h1[:, t, :], bank[i][:, 0:C]).then_inc(copied[i], 1)

            def variance(b, stats, stats_done, m_v, aggregated, v_eps, added):
                dve.wait_ge(stats_done, 4 * (b + 1))
                nc.vector.memset(v_eps, EPS).then_inc(aggregated, 1)
                for t in range(TILES):
                    nc.vector.bn_aggr(m_v[:, t, :], stats[:, t, :]).then_inc(aggregated, 1)
                dve.wait_ge(aggregated, 5 * (b + 1))
                nc.vector.tensor_tensor(v_eps, m_v[:, :, 1], v_eps, ALU.add).then_inc(added, 1)

            def tokens(b, j01, j2, j3):
                for t in range(TILES):
                    if t >= 2:
                        dve.wait_ge(filled[2 + t % 2], (j2, j3)[t % 2] + 1)
                    take(1, PREP[1] + j01 + t, xT[:, t % 2, 4:8, :].rearrange("p k m -> p (k m)"), bank[1][:, :])
                    if t:
                        keep_h(b, t - 1, j2, j3)
                    yield t
                keep_h(b, 3, j2, j3)
                variance(b, stat, stat_done, mean_var, aggr_done, var_eps, eps_added)

            def normalise(b, j2, j3):
                dve.wait_ge(rstd_ready, b + 1)
                dve.wait_ge(copied[2], j2 + 2)
                dve.wait_ge(copied[3], j3 + 2)
                for t in range(TILES):
                    nc.vector.tensor_scalar(xn[:, t, :], h1[:, t, :], mean_var[:, t, 0:1], rstd[:, t:t + 1],
                                            ALU.subtract, ALU.mult).then_inc(xn_ready, 1)

            def project(b, j01, j2, j3, jw, first):
                take(1, PREP[1] + j01, xnT[:, 1, :], bank[1][:, :])
                if not first:
                    dve.wait_ge(k_spread, 64 * b)
                    dve.wait_ge(v_written, 16 * b)
                for half in range(2):
                    dve.wait_ge(filled[6 + half], jw + 1)
                    nc.vector.tensor_scalar(kT[:, half, :], bank[6 + half][:, :], qkv_bc[:, 2 + half:3 + half], None,
                                            ALU.add).then_inc(copied[6 + half], 1)
                for t in range(TILES):
                    i, j = (2, j2) if t % 2 == 0 else (3, j3)
                    dve.wait_ge(filled[i], j + t // 2 + 1)
                    nc.vector.tensor_tensor(v_sb[:, t, :], bank[i][:, 0:C], v_bias, ALU.add).then_inc(copied[i], 1)

            def softmax_rows(b, t, jw):
                dve.wait_ge(filled[4 + t], jw + 1)
                lo = 0 if t == 0 else 2 if t == 3 else 1
                nc.vector.tensor_tensor(score[:, t, :, :].rearrange("p n m -> p (n m)"), bank[4 + t][:, :],
                                        bias_tab[:, lo:lo + 2, :].rearrange("p n m -> p (n m)"), ALU.add).then_inc(copied[4 + t], 1)
                dve.wait_ge(copied[4 + t], jw + 1)
                nc.vector.tensor_reduce(row_max[:, t, :], score[:, t, :, :].rearrange("p n (g r) -> p (n g) r", r=KEYS),
                                        AX.X, ALU.max).then_inc(max_done, 1)

            def row_sums(b, t):
                dve.wait_ge(exp_done, 4 * b + t + 1)
                nc.vector.tensor_reduce(row_sum[:, t, :], score[:, t, :, :].rearrange("p n (g r) -> p (n g) r", r=KEYS),
                                        AX.X, ALU.add).then_inc(sum_done, 1)
                dve.wait_ge(sum_done, 4 * b + t + 1)
                nc.vector.reciprocal(row_inv[:, t, :], row_sum[:, t, :]).then_inc(inv_done, 1)

            def attend(b, j01, j2, j3, jw):
                def probs(t):
                    if t >= 2:
                        dve.wait_ge(filled[4 + t - 2], jw + 1)
                    take(1, PREP[1] + j01 + t // 2, probT[:, t % 2, :, :].rearrange("p n m -> p (n m)"), bank[1][:, :])

                def odds(t):
                    dve.wait_ge(even_done, 4 * b + t + 1)
                    nc.vector.scalar_tensor_tensor(
                        out=att[:, t, :, :].rearrange("p n (m d) -> p (n m) d", d=HD),
                        in0=bank[4 + t].rearrange("p (n a d) -> p n a d", a=2, d=HD)[:, :, 1, :], scalar=parity[:, 1:2],
                        in1=even[:, t % 2, :].rearrange("p (n d) -> p n d", d=HD), op0=ALU.mult, op1=ALU.add).then_inc(copied[4 + t], 1)

                def turned(t):
                    if t >= 2:
                        dve.wait_ge(filled[3], j3 + t - 2 + 1)
                    take(2, j2 + t, attT[:, t % 2, :, :].rearrange("p a (n q) -> p n a q", q=BLK),
                         bank[2][:, 0:256].rearrange("p (n a q) -> p n a q", a=2, q=BLK))

                def residual(t):
                    dve.wait_ge(filled[3], j3 + t + 1)
                    dve.wait_ge(hb_ready, 4 * b + t + 1)
                    nc.vector.tensor_tensor(h2[:, t, :], bank[3][:, 0:C], hb[:, t, :], ALU.add).then_inc(copied[3], 1)
                    dve.wait_ge(copied[3], j3 + t + 1)
                    nc.vector.bn_stats(stat2[:, t, :], h2[:, t, :]).then_inc(stat2_done, 1)

                row_sums(b, 3)
                probs(1)
                odds(0)
                turned(0)
                odds(1)
                probs(3)
                turned(1)
                residual(0)
                odds(2)
                turned(2)
                residual(1)
                odds(3)
                turned(3)
                residual(2)
                residual(3)
                variance(b, stat2, stat2_done, mean_var2, aggr2_done, var_eps2, eps2_added)

            def normalise2(b):
                dve.wait_ge(rstd2_ready, b + 1)
                for t in range(TILES):
                    nc.vector.tensor_scalar(xn2c[:, t, :], h2[:, t, :], mean_var2[:, t, 0:1], rstd2[:, t:t + 1],
                                            ALU.subtract, ALU.mult).then_inc(xn2_ready, 1)

            def route(b, j01, j2):
                take(1, PREP[1] + j01, xn2T[:, 1, :], bank[1][:, :])
                dve.wait_ge(filled[2], j2 + 1)
                by_group = logit.rearrange("p (g t) -> p g t", t=GROUP)
                n = SEQ // GROUP
                nc.vector.tensor_tensor(by_group, bank[2].rearrange("p (g t) -> p g t", t=GROUP),
                                        tie.unsqueeze(1).broadcast_to([P, n, GROUP]), ALU.add).then_inc(copied[2], 1)
                dve.wait_ge(copied[2], j2 + 1)
                nc.vector.tensor_reduce(gmax, by_group, AX.X, ALU.max).then_inc(gmax_done, 1)
                dve.wait_ge(gmax_done, b + 1)
                nc.vector.tensor_tensor(permT[:, bass.ds(SEQ * b, SEQ)].rearrange("p (g t) -> p g t", t=GROUP), by_group,
                                        gmax.unsqueeze(2).broadcast_to([P, n, GROUP]), ALU.is_equal).then_inc(perm_done, 1)

            nc.vector.memset(tab_sb, MASKED).then_inc(tab_masked, 1)
            nc.vector.memset(minus_half, -0.5).then_inc(half_set, 1)
            dve.wait_ge(tok_w_loaded, 32)
            for o in range(2):
                nc.vector.tensor_tensor(w_mix[:, o, :, :], w_sum_sb[:, o, :].unsqueeze(2).broadcast_to([P, C, TAPS]),
                                        w_taps_sb[:, o, :].unsqueeze(1).broadcast_to([P, C, TAPS]), ALU.mult).then_inc(w_mixed, 1)
            dve.wait_ge(ident_ready, 1)
            nc.vector.tensor_reduce(parity[:, :], ident[:, :].rearrange("p (c a q) -> p a c q", c=4, a=2), AX.XY, ALU.add).then_inc(masks_ready, 1)
            nc.vector.tensor_reduce(quarter[:, :], ident[:, :].rearrange("p (c q) -> p c q", c=4), AX.X, ALU.add).then_inc(masks_ready, 1)
            dve.wait_ge(masks_ready, 2)
            dve.wait_ge(vec_loaded, 96)
            nc.vector.tensor_scalar(q_scale, parity[:, :], HD ** -0.5, None, ALU.mult).then_inc(q_consts, 1)
            dve.wait_ge(q_consts, 1)
            for half in range(2):
                nc.vector.tensor_scalar(q_bias[:, half, :], q_scale, qkv_bc[:, half:half + 1], None, ALU.mult).then_inc(q_consts, 1)
            for n in (1, 3):
                take(1, n // 2, w_tok[:, 2 * n:2 * n + 2, :].rearrange("p k o -> p (k o)"), bank[1][:, :])
            weights_qkv(dve, nc.vector.tensor_copy, 1, (1,))
            take(1, 3, w_proj[:, :, :].rearrange("p a o -> p (a o)"), bank[1][:, :])

            for t in tokens(0, 0, 0, 0):
                pass
            normalise(0, 0, 0)
            project(0, 4, 2, 2, 0, True)
            dve.wait_ge(tab_spread, 256)
            with dve.Fori(0, 3) as b:
                j01, j2, j3, jw = jobs_in(b)
                for t in tokens(b + 1, j01, j2, j3):
                    softmax_rows(b, t, jw - 1)
                    if t:
                        row_sums(b, t - 1)
                normalise(b + 1, j2, j3)
                attend(b, j01 + 4, j2 + 2, j3 + 2, jw)
                project(b + 1, j01 + 6, j2 + 6, j3 + 6, jw + 1, False)
                normalise2(b)
                route(b, j01 + 7, j2 + 8)
            for t in range(TILES):
                softmax_rows(3, t, 10)
                if t:
                    row_sums(3, t - 1)
            attend(3, 29, 31, 28, 11)
            normalise2(3)
            route(3, 31, 35)

            with dve.Fori(0, NT // 2) as i2:
                for s in range(2):
                    dve.wait_ge(filled[s], PREP[s] + END01 + i2 + 1)
                    nc.vector.tensor_tensor(perm_bd[:, s, :, :], bank[s][:, 0:P].unsqueeze(1).broadcast_to([P, 4, P]),
                                            quarter[:, :].unsqueeze(2).broadcast_to([P, 4, P]), ALU.mult).then_inc(copied[s], 1)
                for s in range(2):
                    k = 5 + 2 * s
                    dve.wait_ge(filled[k], ENDW + i2 + 1)
                    nc.vector.tensor_copy(dispT[:, 1, :, bass.ds(8 * i2 + 4 * s, 4)],
                                          bank[k].rearrange("p (c e) -> p e c", c=4)).then_inc(copied[k], 1)
            with dve.Fori(0, 2) as i2:
                for s in range(2):
                    dve.wait_ge(filled[4 + s], ENDW + 8 + i2 + 1)
                    g0 = 8 * (2 * i2 + s)
                    nc.vector.tensor_tensor(innerT[:, bass.ds(g0, ROUND), :], bank[4 + s].rearrange("p (g n) -> p g n", g=ROUND),
                                            f_biasT[:, bass.ds(g0, ROUND)].unsqueeze(2).broadcast_to([P, ROUND, NG]),
                                            ALU.add).then_inc(copied[4 + s], 1)
            for u in range(ROUND):
                spread_inner(dve, u, (2, 3), inner_spread_v)
                for i in (1, 3):
                    take_mixed(dve, nc.vector.tensor_copy, u, i)
            dve.wait_ge(h2_done, BATCH)
            for t in range(NT):
                dve.wait_ge(filled[2 + t % 2], COMB0[t % 2] + t // 2 + 1)
                if t >= 4:
                    dve.wait_ge(y_stored[t % 4], 16 * (t // 4))
                nc.vector.tensor_tensor(y_sb[:, t % 4, :], bank[2 + t % 2][:, 0:C], h[:, t, :], ALU.add).then_inc(copied[2 + t % 2], 1)

        @block.gpsimd
        def _(pool):
            def tile_of(tensor, n):
                return tensor[:, bass.ds(n, 1), :].rearrange("p a c -> p (a c)")

            nc.gpsimd.memset(ident[:, :], 0.0).then_inc(ident_zero, 1)
            pool.wait_ge(ident_zero, 1)
            nc.gpsimd.affine_select(out=ident[:, :], in_=ident[:, :], compare_op=ALU.not_equal, fill=1.0, base=0,
                                    pattern=[[-1, P]], channel_multiplier=1).then_inc(ident_ready, 1)

            def power(b, sem_in, src, dst, sem_out):
                pool.wait_ge(sem_in, b + 1)
                nc.gpsimd.tensor_tensor(dst, src, minus_half, ALU.pow).then_inc(sem_out, 1)

            def add_bias(b):
                pool.wait_ge(xn_ready, 4 * (b + 1))
                for t in range(TILES):
                    nc.gpsimd.tensor_tensor(hb[:, t, :], h1[:, t, :], p_bias, ALU.add).then_inc(hb_ready, 1)

            def shift(b, t):
                pool.wait_ge(max_done, 4 * b + t + 1)
                rows = score[:, t, :, :].rearrange("p n (g r) -> p (n g) r", r=KEYS)
                nc.gpsimd.tensor_tensor(rows, rows, row_max[:, t, :].unsqueeze(2).broadcast_to([P, 16, KEYS]),
                                        ALU.subtract).then_inc(shifted, 1)

            def attend(b, jw):
                for t in range(TILES):
                    pool.wait_ge(copied[4 + t], jw + 1)
                    pool.wait_ge(inv_done, 4 * b + t + 1)
                    rows = att[:, t, :, :].rearrange("p n (m d) -> p (n m) d", d=HD)
                    nc.gpsimd.tensor_tensor(rows, rows, row_inv[:, t, :].unsqueeze(2).broadcast_to([P, 16, HD]),
                                            ALU.mult).then_inc(att_scaled, 1)

            def keep(b):
                pool.wait_ge(xn2_ready, 4 * (b + 1))
                nc.gpsimd.tensor_copy(xn2[:, bass.ds(4 * b, 4), :], xn2c[:, :, :]).then_inc(xn2_kept, 1)
                nc.gpsimd.tensor_copy(h[:, bass.ds(4 * b, 4), :], h2[:, :, :]).then_inc(h2_done, 1)

            pool.wait_ge(vec_loaded, 96)
            pool.wait_ge(half_set, 1)
            pool.wait_ge(copied[0], PREP[0])
            pool.wait_ge(copied[1], PREP[1])
            nc.gpsimd.memset(k_bd, 0.0).then_inc(bd_zeroed, 1)
            pool.wait_ge(tab_spread, 256)
            nc.gpsimd.memset(v_bd, 0.0).then_inc(bd_zeroed, 1)
            power(0, eps_added, var_eps, rstd, rstd_ready)
            add_bias(0)
            with pool.Fori(0, 3) as b:
                j01, j2, j3, jw = jobs_in(b)
                for t in range(TILES):
                    shift(b, t)
                power(b + 1, eps_added, var_eps, rstd, rstd_ready)
                attend(b, jw)
                pool.wait_ge(copied[3], j3 + 6)
                add_bias(b + 1)
                power(b, eps2_added, var_eps2, rstd2, rstd2_ready)
                keep(b)
            for t in range(TILES):
                shift(3, t)
            attend(3, 11)
            power(3, eps2_added, var_eps2, rstd2, rstd2_ready)
            keep(3)
            pool.wait_ge(perm_done, BATCH)
            pool.wait_ge(xn2_kept, BATCH)
            with pool.Fori(0, NT // 2) as i2:
                for s in range(2):
                    pool.wait_ge(filled[5 + 2 * s], ENDW + i2)
                    nc.gpsimd.tensor_copy(x_cur[:, s, :], tile_of(xn2, 2 * i2 + s)).then_inc(cur_ready, 1)
                    nc.gpsimd.tensor_copy(perm_cur[:, s, :], permT[:, bass.ds(P * (2 * i2 + s), P)]).then_inc(cur_ready, 1)
            nc.gpsimd.memset(inner_bd, 0.0).then_inc(inner_zeroed, 1)
            pool.wait_ge(filled[7], ENDW + 8)
            for t in range(NT):
                if t >= 2:
                    pool.wait_ge(filled[2 + t % 2], COMB0[t % 2] + (t - 2) // 2 + 1)
                nc.gpsimd.tensor_copy(perm_cur[:, t % 2, :], permT[:, t * P:(t + 1) * P]).then_inc(comb_ready, 1)


_IN = ["x", "L0_tok_weight", "L0_tok_weighted_sum", "L0_attn_qkv_w", "L0_attn_qkv_b", "L0_attn_rpb", "L0_attn_proj_w",
       "L0_attn_proj_b", "L0_ffn_controller", "L0_ffn_f1", "L0_ffn_bias", "L0_ffn_f2"]


def kernel(**inputs):
    import concourse.bacc as bacc
    from concourse.bass_utils import run_bass_kernel_spmd

    nc = bacc.Bacc("TRN2", target_bir_lowering=False, num_devices=1)
    arrays, args = {}, []
    arrays["ties"] = np.float32(1e-6) / np.float32(GROUP - 1) * np.arange(GROUP, dtype=np.float32)
    for name in _IN:
        arrays[name] = np.ascontiguousarray(inputs[name])
        args.append(nc.dram_tensor(name, arrays[name].shape, mybir.dt.from_np(arrays[name].dtype), kind="ExternalInput").ap())
    args.append(nc.dram_tensor("ties", (GROUP,), F32, kind="ExternalInput").ap())
    args.append(nc.dram_tensor("out", (BATCH, SEQ, C), F32, kind="ExternalOutput").ap())
    build(nc, *args)
    r = run_bass_kernel_spmd(nc, [arrays], core_ids=[0])
    return r.results[0]["out"]
```

```python
from contextlib import ExitStack

import numpy as np

import concourse.bass as bass
from concourse import mybir

F32 = mybir.dt.float32
F32R = mybir.dt.float32r
ALU = mybir.AluOpType
ACT = mybir.ActivationFunctionType
AX = mybir.AxisListType

P = 128
BATCH, SEQ, C, TAPS = 4, 512, 256, 4
TILES = SEQ // P
NT = BATCH * TILES
KIN = C * TAPS
HEADS, HD, WIN = 16, 16, 13
RPB = 2 * WIN - 1
BLK = 16
KEYS = 32
NBLK = SEQ // BLK
MASKED = -1.0e38
EPS = 1e-5
GROUP = 32
NG = BATCH * SEQ // GROUP
EXPERTS, FF = 128, 32
ROUND = 8

PREP = (5, 4)
HIGH0 = (4, 3)
SBUF_FROM, SBUF_TO = 2 * 1024, 229344


def key_base(blk):
    return min(max(BLK * blk - 8, 0), SEQ - KEYS)


def neighbourhood(blk, q):
    query = BLK * blk + q
    first = min(max(query - WIN // 2, 0), SEQ - WIN)
    return first - key_base(blk), first - query + WIN - 1


def build(nc, x, w_taps, w_sum, qkv_w, qkv_b, rpb, proj_w, proj_b, controller, f1, f_bias, f2, ties, out):
    x_d = x.rearrange("b (t p) i d -> (b t) p (i d)", p=P)
    out_d = out.rearrange("b (t p) c -> (b t) p c", p=P)
    f1_d = f1.rearrange("(k p) e s f -> p k (e s f)", p=P)
    f2_d = f2.rearrange("e s f d -> (e s f) d")
    v_scratch = nc.dram_tensor("v_scratch", [SEQ, C], F32, kind="Internal").ap()
    tab_scratch = nc.dram_tensor("tab_scratch", [3, 2, BLK, 8, KEYS], F32, kind="Internal").ap()

    with ExitStack() as ctx:
        ctx.enter_context(nc.allow_non_contiguous_dma(reason="small weights and windows"))

        def sem(name):
            return ctx.enter_context(nc.semaphore(name))

        bank = [ctx.enter_context(nc.psum_tensor(f"bank{i}", [P, 512], F32)) for i in range(8)]

        at = [SBUF_FROM]

        def place(name, *shape, dt=F32):
            tensor = nc.alloc_sbuf_tensor_at(name, [P, *shape], dt, offset=at[0])
            at[0] += (4 * int(np.prod(shape)) + 31) // 32 * 32
            assert at[0] <= SBUF_TO, (name, at[0])
            return tensor

        ident = place("ident", P)
        parity = place("parity", 2)
        quarter = place("quarter", 4)
        h = place("h", NT, C)
        xn2 = place("xn2", NT, C)
        permT = place("permT", NT * P)
        f_biasT = place("f_biasT", 32)
        phase_start = at[0]

        x_sb = place("x_sb", TILES, KIN)
        xT_high, xT_low = (place(f"xT_{n}", 2, 8, P, dt=F32R) for n in ("high", "low"))
        w_tok_high, w_tok_low = (place(f"w_tok_{n}", 8, C, dt=F32R) for n in ("high", "low"))
        token_weights_end = at[0]
        w_qkv_high, w_qkv_low = (place(f"w_qkv_{n}", 2, 3 * C, dt=F32R) for n in ("high", "low"))
        ctl_high, ctl_low = (place(f"ctl_{n}", 2, EXPERTS, dt=F32R) for n in ("high", "low"))
        xnT_high, xnT_low = (place(f"xnT_{n}", 2, SEQ, dt=F32R) for n in ("high", "low"))
        w_proj = place("w_proj", 2, C)
        h1 = place("h1", TILES, C)
        h2 = place("h2", TILES, C)
        xn = place("xn", TILES, C)
        q_eo = place("q_eo", 2, NBLK, 2, BLK)
        kT = place("kT", 2, SEQ)
        k_bd_from = at[0]
        k_bd = place("k_bd", 2, 4, SEQ)
        v_sb = place("v_sb", TILES, C)
        v_bd_from = at[0]
        v_bd = place("v_bd", NBLK, 4, 2, 32)
        score = place("score", TILES, 4, P)
        probT = place("probT", 2, 4, P)
        even = place("even", 2, 256)
        att = place("att", TILES, 2, P)
        attT = place("attT", 2, 2, P)
        logit = place("logit", SEQ)
        bias_tab = place("bias_tab", 4, 256)
        v_bias = place("v_bias", C)
        p_bias = place("p_bias", C)
        tie = place("tie", GROUP)
        row_max, row_sum, row_inv = (place(f"row_{n}", TILES, 16) for n in ("max", "sum", "inv"))
        stat, stat2 = (place(n, TILES, 6) for n in ("stat", "stat2"))
        mean_var, mean_var2 = (place(n, TILES, 2) for n in ("mean_var", "mean_var2"))
        var_eps, var_eps2, rstd, rstd2, minus_half = (place(n, TILES) for n in ("var_eps", "var_eps2", "rstd", "rstd2", "minus_half"))
        qkv_bc = place("qkv_bc", 4)
        q_scale = place("q_scale", 2)
        q_bias = place("q_bias", 2, 2)
        gmax = place("gmax", SEQ // GROUP)

        at[0] = k_bd_from
        w_sum_sb = place("w_sum_sb", 2, C)
        w_taps_sb = place("w_taps_sb", 2, TAPS)
        ctl_sb = place("ctl_sb", 2, EXPERTS)
        tab_fill = place("tab_fill", 256)
        at[0] = v_bd_from
        w_mix = place("w_mix", 2, C, TAPS)
        qkv_sb = place("qkv_sb", 6, C)
        proj_sb = place("proj_sb", 2, C)
        f_bias_sb = place("f_bias_sb", P)

        at[0] = phase_start
        f2_sb = place("f2_sb", 32, C)
        f1_early = place("f1_early", 2, 2, 4, ROUND * FF)
        assert at[0] <= token_weights_end
        dispT_from = at[0]
        dispT = place("dispT", 2, EXPERTS, NG)
        at[0] = dispT_from
        interT = place("interT", 2, NG, EXPERTS)
        f1_late = place("f1_late", 2, 2, 4, ROUND * FF)
        innerT = place("innerT", 32, NG)
        inner_bd = place("inner_bd", 2, 4, 4, NG)
        x_cur_high, x_cur_low = (place(f"x_cur_{n}", 4, C, dt=F32R) for n in ("high", "low"))
        perm_bd = place("perm_bd", 2, 4, P, dt=F32R)
        mixed = place("mixed", 2, 4, C)
        y_sb = place("y_sb", 4, C)

        filled = [sem(f"filled{i}") for i in range(8)]
        copied = [sem(f"copied{i}") for i in range(8)]
        x_loaded = [sem(f"x_loaded{i}") for i in range(TILES)]
        ident_zero, ident_ready, masks_ready = sem("ident_zero"), sem("ident_ready"), sem("masks_ready")
        tok_w_loaded, qkv_w_loaded, vec_loaded = sem("tok_w_loaded"), sem("qkv_w_loaded"), sem("vec_loaded")
        ctl_loaded = sem("ctl_loaded")
        w_mixed, q_consts = sem("w_mixed"), sem("q_consts")
        high_done = [sem(f"high_done{i}") for i in range(2)]
        ctl_high_done, ctl_split = sem("ctl_high_done"), sem("ctl_split")
        x_high_done = sem("x_high_done")
        tab_masked, tab_loaded, tab_spread = sem("tab_masked"), sem("tab_loaded"), sem("tab_spread")
        bd_zeroed, half_set = sem("bd_zeroed"), sem("half_set")
        stat_done, aggr_done, eps_added, rstd_ready = (sem(n) for n in ("stat_done", "aggr_done", "eps_added", "rstd_ready"))
        xn_ready, h_biased = sem("xn_ready"), sem("h_biased")
        k_spread, v_written, v_spread = sem("k_spread"), sem("v_written"), sem("v_spread")
        max_done, shifted, exp_done, sum_done, inv_done = (sem(n) for n in ("max_done", "shifted", "exp_done", "sum_done", "inv_done"))
        even_done, att_scaled = sem("even_done"), sem("att_scaled")
        h2_kept, stat2_done, aggr2_done, eps2_added, rstd2_ready = (sem(n) for n in ("h2_kept", "stat2_done", "aggr2_done", "eps2_added", "rstd2_ready"))
        xn2_ready, xn2_kept = sem("xn2_ready"), sem("xn2_kept")
        gmax_done, perm_done = sem("gmax_done"), sem("perm_done")
        cur_ready = sem("cur_ready")
        f1_loaded = [sem(f"f1_loaded{i}") for i in range(4)]
        f2_loaded = sem("f2_loaded")
        inner_zeroed, inner_spread_a, inner_spread_v = sem("inner_zeroed"), sem("inner_spread_a"), sem("inner_spread_v")
        y_stored = [sem(f"y_stored{i}") for i in range(4)]

        block = ctx.enter_context(nc.Block())

        def high_in(b):
            return 5 + 6 * b

        def jobs_in(b):
            return 5 + 8 * b, 4 + 9 * b, 4 + 8 * b, 2 + 3 * b
        END01, END2, END3, ENDW = 32, 36, 32, 12

        MIX0 = [PREP[0] + END01 + 8, PREP[1] + END01 + 8, END2, END3] + [ENDW + 8 + 2, ENDW + 8 + 2, ENDW + 8, ENDW + 8]
        COMB0 = [n + 4 for n in MIX0]

        @block.sync
        def _(sp):
            def load_x(b, waits):
                for t in range(TILES):
                    if waits is not None:
                        sp.wait_ge(copied[1], waits + t + 1)
                    sp.dma_start(x_sb[:, t, :], x_d[4 * b + t, :, :] if isinstance(b, int) else
                                 x_d[bass.ds(4 * b + t, 1), :, :].rearrange("a p n -> (a p) n")).then_inc(x_loaded[t], 16)

            def spread_kv(b, jw, j2, j3, first):
                for i in (6, 7):
                    sp.wait_ge(copied[i], jw + 1)
                for g in range(4):
                    sp.dma_start(k_bd[32 * g:32 * g + 32, :, g, :], kT[32 * g:32 * g + 32, :, :]).then_inc(k_spread, 16)
                sp.wait_ge(copied[2], j2)
                sp.wait_ge(copied[3], j3)
                if not first:
                    sp.wait_ge(v_spread, 128 * b)
                sp.dma_start(v_scratch.rearrange("(t p) c -> p t c", p=P), v_sb[:, :, :]).then_inc(v_written, 16)
                sp.wait_ge(v_written, 16 * (b + 1))
                for g in range(4):
                    rows = slice(32 * g, 32 * g + 32)
                    inner = bass.AP(v_scratch.tensor, (BLK - 8) * C + 64 * g, [[C, KEYS], [BLK * C, NBLK - 2], [1, 64]])
                    edges = bass.AP(v_scratch.tensor, 64 * g, [[C, KEYS], [(SEQ - KEYS) * C, 2], [1, 64]])
                    v4 = v_bd[rows, :, g, :, :].rearrange("p n a c -> p n (a c)")
                    sp.dma_start(v4[:, 1:NBLK - 1, :], inner).then_inc(v_spread, 16)
                    sp.dma_start(v4[:, 0:NBLK:NBLK - 1, :], edges).then_inc(v_spread, 16)

            sp.dma_start(w_sum_sb[:, :, :], w_sum.rearrange("(o p) i -> p o i", p=P)).then_inc(tok_w_loaded, 16)
            sp.dma_start(w_taps_sb[:, :, :], w_taps.rearrange("(o p) d -> p o d", p=P)).then_inc(tok_w_loaded, 16)
            load_x(0, None)
            sp.dma_start(qkv_sb[:, :, :], qkv_w.rearrange("(r p) c -> p r c", p=P)).then_inc(qkv_w_loaded, 16)
            for r in range(2):
                for a in range(2):
                    sp.dma_start(proj_sb[:, r, a * P:(a + 1) * P].rearrange("p (n d) -> p n d", d=HD),
                                 proj_w[r * P:(r + 1) * P, :].rearrange("p (n a d) -> p a n d", a=2, d=HD)[:, a, :, :]).then_inc(qkv_w_loaded, 16)
            sp.dma_start(f_bias_sb[0:32, :].rearrange("g (j f) -> g j f", j=4),
                         f_bias.rearrange("e s f -> (e s f)").rearrange("(j g f) -> g j f", j=4, g=32)).then_inc(qkv_w_loaded, 16)
            sp.wait_ge(tab_masked, 1)
            sp.dma_start(tab_scratch.rearrange("v a q n r -> (v a q) (n r)"), tab_fill[0:96, :]).then_inc(tab_loaded, 16)
            sp.dma_start(ctl_sb[:, :, :], controller.rearrange("(k p) e s -> p k (e s)", p=P)).then_inc(ctl_loaded, 16)
            sp.dma_start(qkv_bc[:, :], qkv_b.rearrange("(r p) -> p r", p=P)[:, 0:4]).then_inc(vec_loaded, 16)
            for a in range(2):
                sp.dma_start(v_bias[:, :].rearrange("p (g a c) -> p a g c", g=4, a=2)[:, a, :, :],
                             bass.AP(qkv_b.tensor, 2 * C + 128 * a, [[0, P], [32, 4], [1, 32]])).then_inc(vec_loaded, 16)
            sp.dma_start(p_bias[:, :], bass.AP(proj_b.tensor, 0, [[0, P], [1, C]])).then_inc(vec_loaded, 16)
            sp.dma_start(tie[:, :], bass.AP(ties.tensor, 0, [[0, P], [1, GROUP]])).then_inc(vec_loaded, 16)
            sp.wait_ge(tab_loaded, 16)
            runs = 0
            for v, blk in enumerate((0, 1, NBLK - 1)):
                q = 0
                while q < BLK:
                    (r0, s0), n = neighbourhood(blk, q), 1
                    while q + n < BLK and neighbourhood(blk, q + n) == (r0 + n, s0):
                        n += 1
                    row = (v * 2 * BLK + q) * 256 + r0
                    if n == 1:
                        pairs = [(bass.AP(tab_scratch.tensor, row, [[BLK * 256, 2], [KEYS, 8], [1, WIN]]),
                                  bass.AP(rpb.tensor, s0, [[RPB, 2], [2 * RPB, 8], [1, WIN]]))]
                    else:
                        pairs = [(bass.AP(tab_scratch.tensor, row + par * BLK * 256, [[256 + 1, n], [KEYS, 8], [1, WIN]]),
                                  bass.AP(rpb.tensor, par * RPB + s0, [[0, n], [2 * RPB, 8], [1, WIN]])) for par in range(2)]
                    for dst, src in pairs:
                        sp.dma_start(dst, src).then_inc(tab_loaded, 16)
                        runs += 1
                    q += n
            sp.wait_ge(tab_loaded, 16 * (1 + runs))
            for quad in range(4):
                sp.dma_start(bias_tab[:, quad, :], bass.AP(tab_scratch.tensor, 32 * 256, [[0, 4], [256, 32], [1, 256]])).then_inc(tab_spread, 16)
            sp.wait_ge(tab_spread, 64)
            sp.dma_start(bias_tab[0:32, 0, :], bass.AP(tab_scratch.tensor, 0, [[256, 32], [1, 256]])).then_inc(tab_spread, 16)
            sp.dma_start(bias_tab[96:128, 3, :], bass.AP(tab_scratch.tensor, 2 * 32 * 256, [[256, 32], [1, 256]])).then_inc(tab_spread, 16)
            load_x(1, PREP[1])
            sp.wait_ge(bd_zeroed, 2)
            spread_kv(0, 0, 4, 4, True)
            with sp.Fori(0, 2) as b:
                j01, j2, j3, jw = jobs_in(b)
                load_x(b + 2, PREP[1] + j01)
                spread_kv(b + 1, jw + 1, j2 + 8, j3 + 8, False)
            j01, j2, j3, jw = jobs_in(2)
            sp.wait_ge(filled[2], j2 + 2)
            sp.wait_ge(filled[3], j3 + 2)
            for j in range(4):
                sp.dma_start(f2_sb[32 * j:32 * j + 32, :, :],
                             f2_d.rearrange("(j g f) d -> j f g d", j=4, g=32)[j]).then_inc(f2_loaded, 16)
            spread_kv(3, jw + 1, j2 + 8, j3 + 8, False)

            def load_f1(f1_sb, rounds):
                for rnd in rounds:
                    for k in range(2):
                        sp.dma_start(f1_sb[:, rnd % 2, k, :, :], f1_d.rearrange("p k (j g n) -> p k j g n", j=4, g=4)
                                     [:, k, :, rnd, :]).then_inc(f1_loaded[rnd], 16)

            load_f1(f1_early, (0, 1))
            sp.wait_ge(perm_done, BATCH)
            sp.wait_ge(h2_kept, BATCH)
            load_f1(f1_late, (2, 3))
            for t in range(NT):
                sp.wait_ge(copied[2 + t % 2], COMB0[2 + t % 2] + t // 2 + 1)
                sp.dma_start(out_d[t], y_sb[:, t % 4, :]).then_inc(y_stored[t % 4], 16)
            for s in range(4):
                sp.wait_ge(y_stored[s], 16 * (NT // 4))

        @block.tensor
        def _(pe):
            def room(i, job):
                if not (isinstance(job, int) and job == 0):
                    pe.wait_ge(copied[i], job)

            def turn4(i, job, sources):
                room(i, job)
                n = 0
                for s in sources:
                    k, m = s.shape[0], int(np.prod(s.shape[1:]))
                    last = nc.tensor.transpose(bank[i][0:m, n:n + k], s, ident[0:k, 0:k])
                    n += k
                last.then_inc(filled[i], 1)

            def products(out, terms):
                passes = [(lh, rh) for lh, ll, rh, rl in terms] + [(lh, rl) for lh, ll, rh, rl in terms] + \
                         [(ll, rh) for lh, ll, rh, rl in terms]
                for n, (lhs, rhs) in enumerate(passes):
                    last = nc.tensor.matmul(out, lhs, rhs, start=(n == 0), stop=(n == len(passes) - 1))
                return last

            def weights():
                pe.wait_ge(ident_ready, 1)
                pe.wait_ge(w_mixed, 2)
                for n in range(4):
                    turn4(n % 2, n // 2, [w_mix[:, :, :, :].rearrange("p o i d -> p o (i d)")[:, o, k * P:(k + 1) * P]
                                          for k in (2 * n, 2 * n + 1) for o in range(2)])
                pe.wait_ge(qkv_w_loaded, 96)
                for n in range(3):
                    turn4(n % 2, 2 + n // 2, [qkv_sb[:, r, k * P:(k + 1) * P] for r in (2 * n, 2 * n + 1) for k in range(2)])
                turn4(1, 3, [proj_sb[:, o, a * P:(a + 1) * P] for a in range(2) for o in range(2)])
                turn4(0, 4, [f_bias_sb[0:32, :]])

            def turn_x(b, t, j01):
                pe.wait_ge(x_loaded[t], 16 * (b + 1))
                for i in range(2):
                    turn4(i, PREP[i] + j01 + t, [x_sb[:, t, (4 * i + k) * P:(4 * i + k + 1) * P] for k in range(4)])

            def token_products(t, j01, j2, j3):
                i, j = (2, j2) if t % 2 == 0 else (3, j3)
                pe.wait_ge(copied[0], PREP[0] + j01 + t + 1)
                pe.wait_ge(copied[1], PREP[1] + j01 + t + 1)
                room(i, j + t // 2)
                s = t % 2
                products(bank[i][:, 0:C], [(xT_high[:, s, k, :], xT_low[:, s, k, :], w_tok_high[:, k, :], w_tok_low[:, k, :])
                                           for k in range(8)]).then_inc(filled[i], 1)

            def turn_xn(b, j01, ready):
                pe.wait_ge(ready, 4 * (b + 1))
                for i in range(2):
                    turn4(i, PREP[i] + j01, [xn[:, t, i * P:(i + 1) * P] for t in range(TILES)])

            def wide(r, j01, jw):
                if r == 2:
                    for i in range(2):
                        pe.wait_ge(copied[i], PREP[i] + j01 + 1)
                room(4 + r, jw)
                products(bank[4 + r][:, :], [(w_qkv_high[:, k, r * P:(r + 1) * P], w_qkv_low[:, k, r * P:(r + 1) * P],
                                              xnT_high[:, k, :], xnT_low[:, k, :]) for k in range(2)]).then_inc(filled[4 + r], 1)

            def value_rows(t, j2, j3):
                i, j = (2, j2) if t % 2 == 0 else (3, j3)
                room(i, j + t // 2)
                products(bank[i][:, 0:C], [(xnT_high[:, k, t * P:(t + 1) * P], xnT_low[:, k, t * P:(t + 1) * P],
                                            w_qkv_high[:, k, 2 * C:3 * C], w_qkv_low[:, k, 2 * C:3 * C])
                                           for k in range(2)]).then_inc(filled[i], 1)

            def scores(b, jw):
                pe.wait_ge(k_spread, 64 * (b + 1))
                for i in (4, 5):
                    pe.wait_ge(copied[i], jw)
                for t in range(TILES):
                    room(4 + t, jw)
                    for n in range(4):
                        for c in range(4):
                            blk, half = 8 * t + 4 * (n // 2) + c, n % 2
                            last = nc.tensor.matmul(bank[4 + t][32 * c:32 * c + 32, n * P:(n + 1) * P],
                                                    q_eo[:, half, blk, :, :].rearrange("p a q -> p (a q)"),
                                                    k_bd[:, half, :, key_base(blk):key_base(blk) + KEYS],
                                                    start=True, stop=True, tile_position=(0, 32 * c))
                    last.then_inc(filled[4 + t], 1)

            def turn_probs(b, t, j01):
                pe.wait_ge(exp_done, 4 * b + t + 1)
                turn4(t % 2, PREP[t % 2] + j01 + t // 2, [score[:, t, n, :] for n in range(4)])

            def values(b, t, j01, jw):
                pe.wait_ge(copied[t % 2], PREP[t % 2] + j01 + t // 2 + 1)
                if t == 0:
                    pe.wait_ge(v_spread, 128 * (b + 1))
                room(4 + t, jw)
                for n in range(4):
                    for c in range(4):
                        blk, half = 8 * t + 4 * (n // 2) + c, n % 2
                        last = nc.tensor.matmul(bank[4 + t][32 * c:32 * c + 32, n * P:(n + 1) * P],
                                                probT[:, t % 2, n, 32 * c:32 * c + 32], v_bd[:, blk, :, half, :],
                                                start=True, stop=True, tile_position=(0, 32 * c))
                last.then_inc(filled[4 + t], 1)

            def turn_att(b, t, j2):
                pe.wait_ge(att_scaled, 4 * b + t + 1)
                turn4(2, j2 + t, [att[:, t, n, :] for n in range(2)])

            def out_proj(t, j2, j3):
                pe.wait_ge(copied[2], j2 + t + 1)
                room(3, j3 + t)
                for a in range(2):
                    last = nc.tensor.matmul(bank[3][:, 0:C], attT[:, t % 2, a, :], w_proj[:, a, :], start=(a == 0), stop=(a == 1))
                last.then_inc(filled[3], 1)

            def route(b, j01, j2):
                turn_xn(b, j01, xn2_ready)
                for i in range(2):
                    pe.wait_ge(copied[i], PREP[i] + j01 + 1)
                room(2, j2)
                products(bank[2][:, :], [(ctl_high[:, k, :], ctl_low[:, k, :], xnT_high[:, k, :], xnT_low[:, k, :])
                                         for k in range(2)]).then_inc(filled[2], 1)

            weights()
            pe.wait_ge(copied[0], PREP[0])
            pe.wait_ge(copied[1], PREP[1])
            for t in range(TILES):
                turn_x(0, t, 0)
                if t:
                    token_products(t - 1, 0, 0, 0)
            token_products(3, 0, 0, 0)
            turn_xn(0, 4, xn_ready)
            for r in (2, 3, 0, 1):
                wide(r, 4, 0)
            for t in range(TILES):
                value_rows(t, 2, 2)
            scores(0, 1)
            with pe.Fori(0, 3) as b:
                j01, j2, j3, jw = jobs_in(b)
                ja, j2a, j3a = j01 + 4, j2 + 2, j3 + 2
                turn_x(b + 1, 0, j01)
                turn_x(b + 1, 1, j01)
                token_products(0, j01, j2, j3)
                turn_x(b + 1, 2, j01)
                token_products(1, j01, j2, j3)
                turn_x(b + 1, 3, j01)
                turn_probs(b, 0, ja)
                token_products(2, j01, j2, j3)
                turn_probs(b, 1, ja)
                values(b, 0, ja, jw)
                token_products(3, j01, j2, j3)
                turn_probs(b, 2, ja)
                values(b, 1, ja, jw)
                turn_att(b, 0, j2a)
                turn_probs(b, 3, ja)
                values(b, 2, ja, jw)
                turn_att(b, 1, j2a)
                out_proj(0, j2a, j3a)
                values(b, 3, ja, jw)
                turn_xn(b + 1, ja + 2, xn_ready)
                turn_att(b, 2, j2a)
                out_proj(1, j2a, j3a)
                wide(2, ja + 2, jw + 1)
                turn_att(b, 3, j2a)
                out_proj(2, j2a, j3a)
                wide(3, ja + 2, jw + 1)
                out_proj(3, j2a, j3a)
                wide(0, ja + 2, jw + 1)
                wide(1, ja + 2, jw + 1)
                for t in range(TILES):
                    value_rows(t, j2 + 6, j3 + 6)
                route(b, ja + 3, j2 + 8)
                scores(b + 1, jw + 2)
            turn_probs(3, 0, 29)
            turn_probs(3, 1, 29)
            values(3, 0, 29, 11)
            turn_probs(3, 2, 29)
            values(3, 1, 29, 11)
            turn_att(3, 0, 31)
            turn_probs(3, 3, 29)
            values(3, 2, 29, 11)
            turn_att(3, 1, 31)
            out_proj(0, 31, 28)
            values(3, 3, 29, 11)
            turn_att(3, 2, 31)
            out_proj(1, 31, 28)
            turn_att(3, 3, 31)
            out_proj(2, 31, 28)
            out_proj(3, 31, 28)
            route(3, 31, 35)

            def turn_perm(t):
                turn4(t % 2, PREP[t % 2] + END01 + t // 2, [permT[:, t * P:(t + 1) * P]])

            pe.wait_ge(perm_done, BATCH)
            turn_perm(0)
            for t in range(NT):
                if t + 1 < NT:
                    turn_perm(t + 1)
                pe.wait_ge(copied[t % 2], PREP[t % 2] + END01 + t // 2 + 1)
                pe.wait_ge(cur_ready, t + 1)
                for half in range(2):
                    k = 4 + 2 * (t % 2) + half
                    room(k, ENDW + t // 2)
                    cols = slice(half * P, (half + 1) * P)
                    nc.tensor.matmul(bank[k][:, :], x_cur_high[:, t % 4, cols], perm_bd[:, t % 2, :, :], start=True, stop=False)
                    nc.tensor.matmul(bank[k][:, :], x_cur_low[:, t % 4, cols], perm_bd[:, t % 2, :, :],
                                     start=False, stop=True).then_inc(filled[k], 1)
            for k in range(4, 8):
                pe.wait_ge(copied[k], ENDW + 8)
            for rnd in range(4):
                s = rnd % 2
                pe.wait_ge(f1_loaded[rnd], 32)
                room(4 + s, ENDW + 8 + rnd // 2)
                for g in range(ROUND):
                    for k in range(2):
                        for j in range(4):
                            last = nc.tensor.matmul(bank[4 + s][32 * j:32 * j + 32, g * NG:(g + 1) * NG],
                                                    (f1_early, f1_late)[rnd // 2][:, s, k, j, g * FF:(g + 1) * FF],
                                                    dispT[:, k, 32 * j + 8 * rnd + g, :],
                                                    start=(k == 0), stop=(k == 1), tile_position=(0, 32 * j))
                last.then_inc(filled[4 + s], 1)
            pe.wait_ge(f2_loaded, 64)
            for u in range(ROUND):
                pe.wait_ge(inner_spread_a, 2 * (u + 1))
                pe.wait_ge(inner_spread_v, 2 * (u + 1))
                for i in range(4):
                    s = 4 * (u % 2) + i
                    room(s, MIX0[s] + u // 2)
                    for half in range(2):
                        last = nc.tensor.matmul(bank[s][:, half * C:(half + 1) * C], f2_sb[:, 8 * i + u, half * P:(half + 1) * P],
                                                inner_bd[:, u % 2, i, :, :], start=True, stop=True)
                    last.then_inc(filled[s], 1)
            def turn_mixed(t):
                for a in range(2):
                    i = 4 * (t % 2) + a
                    turn4(i, COMB0[i] + t // 2, [interT[:, half, 4 * t + c, :] for c in (2 * a, 2 * a + 1) for half in range(2)])

            for s in range(8):
                pe.wait_ge(copied[s], COMB0[s])
            turn_mixed(0)
            for t in range(NT):
                if t + 1 < NT:
                    turn_mixed(t + 1)
                for a in range(2):
                    pe.wait_ge(copied[4 * (t % 2) + a], COMB0[4 * (t % 2) + a] + t // 2 + 1)
                room(2 + t % 2, COMB0[2 + t % 2] + t // 2)
                for c in range(4):
                    last = nc.tensor.matmul(bank[2 + t % 2][32 * c:32 * c + 32, 0:C], permT[:, (4 * t + c) * 32:(4 * t + c + 1) * 32],
                                            mixed[:, t % 2, c, :], start=True, stop=True, tile_position=(0, 32 * c))
                last.then_inc(filled[2 + t % 2], 1)

        def weights_qkv(src, parts, n, put):
            view = src.rearrange("p (r k o) -> p r k o", r=2, k=2)
            for r in range(2):
                if n < 2:
                    pick = [w[:, :, (2 * n + r) * P:(2 * n + r + 1) * P] for w in parts]
                    last = put(pick, view[:, r, :, :])
                else:
                    pick = [w[:, :, 2 * C:3 * C].rearrange("p k (g a c) -> p a k g c", g=4, a=2)[:, r, :, :, :] for w in parts]
                    last = put(pick, view[:, r, :, :].rearrange("p k (g c) -> p k g c", g=4))
            return last

        def spread_inner(eng, u, js, done):
            if u == 0:
                for k in (4, 5):
                    eng.wait_ge(copied[k], ENDW + 8 + 2)
                eng.wait_ge(inner_zeroed, 1)
            if u >= 2:
                for s in range(4 * (u % 2), 4 * (u % 2) + 4):
                    eng.wait_ge(filled[s], MIX0[s] + (u - 2) // 2 + 1)
            for j in js:
                rows = slice(32 * j, 32 * j + 32)
                dst, src = inner_bd[rows, u % 2, :, j, :], innerT[rows, u:32:ROUND, :]
                if done is inner_spread_a:
                    nc.scalar.activation(dst, src, ACT.Relu).then_inc(done, 1)
                else:
                    nc.vector.tensor_scalar(dst, src, 0.0, None, ALU.max).then_inc(done, 1)

        def take_mixed(eng, copy, u, i):
            s = 4 * (u % 2) + i
            eng.wait_ge(filled[s], MIX0[s] + u // 2 + 1)
            dst = interT[:, :, :, 8 * i + u:EXPERTS:32].rearrange("p a g j -> p a j g")
            src = bank[s].rearrange("p (a j g) -> p a j g", a=2, j=4)
            copy(dst, src).then_inc(copied[s], 1)

        def batch_of(tensor, b):
            return tensor[:, bass.ds(4 * b, 4), :]

        def tile_of(tensor, n):
            return tensor[:, bass.ds(n, 1), :].rearrange("p a c -> p (a c)")

        def flat(ap):
            return ap.rearrange("p a b -> p (a b)")

        @block.scalar
        def _(act):
            def take(i, job, dst, src):
                act.wait_ge(filled[i], job + 1)
                nc.scalar.copy(dst, src).then_inc(copied[i], 1)

            def high(i, job, dst):
                act.wait_ge(filled[i], job + 1)
                nc.scalar.copy(dst, bank[i][:, :]).then_inc(high_done[i], 1)

            def take_x(t, j01, j2, j3):
                if t >= 2:
                    act.wait_ge(filled[2 + t % 2], (j2, j3)[t % 2] + 1)
                for i in range(2):
                    high(i, PREP[i] + j01 + t, flat(xT_high[:, t % 2, 4 * i:4 * i + 4, :]))

            def exps(b, t):
                act.wait_ge(shifted, 4 * b + t + 1)
                nc.scalar.activation(score[:, t, :, :], score[:, t, :, :], ACT.Exp).then_inc(exp_done, 1)

            def take_xn(j01):
                for i in range(2):
                    high(i, PREP[i] + j01, xnT_high[:, i, :])

            def queries(half, jw):
                act.wait_ge(filled[4 + half], jw + 1)
                for a in range(2):
                    last = nc.scalar.activation(q_eo[:, half, :, a, :], bank[4 + half].rearrange("p (n q) -> p n q", q=BLK), ACT.Identity,
                                                bias=q_bias[:, half, a:a + 1], scale=q_scale[:, a:a + 1])
                last.then_inc(copied[4 + half], 1)

            def probs(t, j01, jw):
                if t >= 2:
                    act.wait_ge(filled[4 + t - 2], jw + 1)
                take(t % 2, PREP[t % 2] + j01 + t // 2, flat(probT[:, t % 2, :, :]), bank[t % 2][:, :])

            def evens(t, jw):
                act.wait_ge(filled[4 + t], jw + 1)
                if t >= 2:
                    act.wait_ge(copied[4 + t - 2], jw + 1)
                nc.scalar.mul(even[:, t % 2, :].rearrange("p (n d) -> p n d", d=HD),
                              bank[4 + t].rearrange("p (n a d) -> p n a d", a=2, d=HD)[:, :, 0, :],
                              parity[:, 0:1]).then_inc(even_done, 1)

            for n in range(4):
                high(n % 2, n // 2, flat(w_tok_high[:, 2 * n:2 * n + 2, :]))
            for n in range(3):
                act.wait_ge(filled[n % 2], 3 + n // 2)
                weights_qkv(bank[n % 2], [w_qkv_high], n, lambda dst, src: nc.scalar.copy(dst[0], src)).then_inc(high_done[n % 2], 1)
            take(1, 3, flat(w_proj[:, :, :]), bank[1][:, :])
            take(0, 4, f_biasT[:, :], bank[0][:, 0:32])
            act.wait_ge(ctl_loaded, 16)
            nc.scalar.copy(ctl_high[:, :, :], ctl_sb[:, :, :]).then_inc(ctl_high_done, 1)
            for t in range(TILES):
                take_x(t, 0, 0, 0)
            take_xn(4)
            act.wait_ge(q_consts, 3)
            queries(0, 0)
            queries(1, 0)
            with act.Fori(0, 3) as b:
                j01, j2, j3, jw = jobs_in(b)
                ja = j01 + 4
                take_x(0, j01, j2, j3)
                take_x(1, j01, j2, j3)
                exps(b, 0)
                take_x(2, j01, j2, j3)
                exps(b, 1)
                take_x(3, j01, j2, j3)
                exps(b, 2)
                probs(0, ja, jw)
                exps(b, 3)
                probs(1, ja, jw)
                evens(0, jw)
                probs(2, ja, jw)
                evens(1, jw)
                probs(3, ja, jw)
                evens(2, jw)
                evens(3, jw)
                take_xn(ja + 2)
                queries(0, jw + 1)
                queries(1, jw + 1)
                take_xn(ja + 3)
            for t in range(TILES):
                exps(3, t)
            for t in (0, 1):
                probs(t, 29, 11)
            evens(0, 11)
            probs(2, 29, 11)
            evens(1, 11)
            probs(3, 29, 11)
            evens(2, 11)
            evens(3, 11)
            take_xn(31)
            act.wait_ge(perm_done, BATCH)
            act.wait_ge(h2_kept, BATCH)
            with act.Fori(0, NT // 2) as i2:
                for s in range(2):
                    for half in range(2):
                        k = 4 + 2 * s + half
                        act.wait_ge(filled[k], ENDW + i2 + 1)
                        nc.scalar.copy(dispT[:, half, :, bass.ds(8 * i2 + 4 * s, 4)],
                                       bank[k].rearrange("p (c e) -> p e c", c=4)).then_inc(copied[k], 1)
            for u in (0, 1):
                spread_inner(act, u, (0, 1), inner_spread_a)
            for u in range(ROUND):
                for i in (0, 2):
                    take_mixed(act, nc.scalar.copy, u, i)
                if u + 2 < ROUND:
                    spread_inner(act, u + 2, (0, 1), inner_spread_a)
            with act.Fori(0, NT // 2) as i2:
                for s in range(2):
                    act.wait_ge(filled[2 + s], COMB0[2 + s] + i2)
                    take(4 * s, COMB0[4 * s] + i2, flat(mixed[:, s, 0:2, :]), bank[4 * s][:, :])

        @block.vector
        def _(dve):
            def low(i, n, dst, high_part):
                dve.wait_ge(high_done[i], n + 1)
                nc.vector.tensor_tensor(dst, bank[i][:, :], high_part.bitcast(F32), ALU.subtract).then_inc(copied[i], 1)

            def take_x(t, n):
                for i in range(2):
                    ks = slice(4 * i, 4 * i + 4)
                    low(i, HIGH0[i] + n + t, flat(xT_low[:, t % 2, ks, :]), flat(xT_high[:, t % 2, ks, :]))

            def keep_h(b, t, j2, j3):
                i, j = (2, j2) if t % 2 == 0 else (3, j3)
                if t == 0 and not (isinstance(b, int) and b == 0):
                    dve.wait_ge(h_biased, 4 * b)
                dve.wait_ge(filled[i], j + t // 2 + 1)
                nc.vector.bn_stats(stat[:, t, :], bank[i][:, 0:C]).then_inc(stat_done, 1)
                nc.vector.tensor_copy(h1[:, t, :], bank[i][:, 0:C]).then_inc(copied[i], 1)

            def variance(b, stats, stats_done, m_v, aggregated, v_eps, added):
                dve.wait_ge(stats_done, 4 * (b + 1))
                nc.vector.memset(v_eps[:, :], EPS).then_inc(aggregated, 1)
                for t in range(TILES):
                    nc.vector.bn_aggr(m_v[:, t, :], stats[:, t, :]).then_inc(aggregated, 1)
                dve.wait_ge(aggregated, 5 * (b + 1))
                nc.vector.tensor_tensor(v_eps[:, :], m_v[:, :, 1], v_eps[:, :], ALU.add).then_inc(added, 1)

            def normalise(b, rows, m_v, inv, inv_ready, done):
                dve.wait_ge(inv_ready, b + 1)
                for t in range(TILES):
                    nc.vector.tensor_scalar(xn[:, t, :], rows[:, t, :], m_v[:, t, 0:1], inv[:, t:t + 1],
                                            ALU.subtract, ALU.mult).then_inc(done, 1)

            def first_variance(b, j2, j3):
                dve.wait_ge(copied[2], j2 + 2)
                dve.wait_ge(copied[3], j3 + 2)
                variance(b, stat, stat_done, mean_var, aggr_done, var_eps, eps_added)

            def first_norm(b):
                normalise(b, h1, mean_var, rstd, rstd_ready, xn_ready)

            def take_xn(n):
                for i in range(2):
                    low(i, HIGH0[i] + n, xnT_low[:, i, :], xnT_high[:, i, :])

            def keys(b, half, jw, first):
                if half == 0 and not first:
                    dve.wait_ge(k_spread, 64 * b)
                    dve.wait_ge(v_written, 16 * b)
                dve.wait_ge(filled[6 + half], jw + 1)
                nc.vector.tensor_scalar(kT[:, half, :], bank[6 + half][:, :], qkv_bc[:, 2 + half:3 + half], None,
                                        ALU.add).then_inc(copied[6 + half], 1)

            def value_rows(t, j2, j3):
                i, j = (2, j2) if t % 2 == 0 else (3, j3)
                dve.wait_ge(filled[i], j + t // 2 + 1)
                nc.vector.tensor_tensor(v_sb[:, t, :], bank[i][:, 0:C], v_bias[:, :], ALU.add).then_inc(copied[i], 1)

            def rows_of(t):
                return score[:, t, :, :].rearrange("p n (g r) -> p (n g) r", r=KEYS)

            def row_maxima(b, t, jw):
                dve.wait_ge(filled[4 + t], jw + 1)
                lo = 0 if t == 0 else 2 if t == 3 else 1
                nc.vector.tensor_tensor(flat(score[:, t, :, :]), bank[4 + t][:, :],
                                        flat(bias_tab[:, lo:lo + 2, :]), ALU.add).then_inc(copied[4 + t], 1)
                dve.wait_ge(copied[4 + t], jw + 1)
                nc.vector.tensor_reduce(row_max[:, t, :], rows_of(t), AX.X, ALU.max).then_inc(max_done, 1)

            def row_sums(b, t):
                dve.wait_ge(exp_done, 4 * b + t + 1)
                nc.vector.tensor_reduce(row_sum[:, t, :], rows_of(t), AX.X, ALU.add).then_inc(sum_done, 1)
                dve.wait_ge(sum_done, 4 * b + t + 1)
                nc.vector.reciprocal(row_inv[:, t, :], row_sum[:, t, :]).then_inc(inv_done, 1)

            def odds(b, t):
                dve.wait_ge(even_done, 4 * b + t + 1)
                nc.vector.scalar_tensor_tensor(
                    out=att[:, t, :, :].rearrange("p n (m d) -> p (n m) d", d=HD),
                    in0=bank[4 + t].rearrange("p (n a d) -> p n a d", a=2, d=HD)[:, :, 1, :], scalar=parity[:, 1:2],
                    in1=even[:, t % 2, :].rearrange("p (n d) -> p n d", d=HD), op0=ALU.mult, op1=ALU.add).then_inc(copied[4 + t], 1)

            def turned(t, j2, j3):
                if t >= 2:
                    dve.wait_ge(filled[3], j3 + t - 2 + 1)
                dve.wait_ge(filled[2], j2 + t + 1)
                nc.vector.tensor_copy(attT[:, t % 2, :, :].rearrange("p a (n q) -> p n a q", q=BLK),
                                      bank[2][:, 0:256].rearrange("p (n a q) -> p n a q", a=2, q=BLK)).then_inc(copied[2], 1)

            def residual(b, t, j3):
                dve.wait_ge(filled[3], j3 + t + 1)
                dve.wait_ge(h_biased, 4 * b + t + 1)
                nc.vector.tensor_tensor(h2[:, t, :], bank[3][:, 0:C], tile_of(h, 4 * b + t), ALU.add).then_inc(copied[3], 1)
                dve.wait_ge(copied[3], j3 + t + 1)
                nc.vector.bn_stats(stat2[:, t, :], h2[:, t, :]).then_inc(stat2_done, 1)

            def second_norm(b):
                normalise(b, h2, mean_var2, rstd2, rstd2_ready, xn2_ready)

            def route(b, n, j2):
                take_xn(n)
                dve.wait_ge(filled[2], j2 + 1)
                by_group = logit[:, :].rearrange("p (g t) -> p g t", t=GROUP)
                groups = SEQ // GROUP
                nc.vector.tensor_tensor(by_group, bank[2].rearrange("p (g t) -> p g t", t=GROUP),
                                        tie[:, :].unsqueeze(1).broadcast_to([P, groups, GROUP]), ALU.add).then_inc(copied[2], 1)
                dve.wait_ge(copied[2], j2 + 1)
                nc.vector.tensor_reduce(gmax[:, :], by_group, AX.X, ALU.max).then_inc(gmax_done, 1)
                dve.wait_ge(gmax_done, b + 1)
                nc.vector.tensor_tensor(permT[:, bass.ds(SEQ * b, SEQ)].rearrange("p (g t) -> p g t", t=GROUP), by_group,
                                        gmax[:, :].unsqueeze(2).broadcast_to([P, groups, GROUP]), ALU.is_equal).then_inc(perm_done, 1)

            nc.vector.memset(tab_fill[:, :], MASKED).then_inc(tab_masked, 1)
            nc.vector.memset(minus_half[:, :], -0.5).then_inc(half_set, 1)
            dve.wait_ge(tok_w_loaded, 32)
            for o in range(2):
                nc.vector.tensor_tensor(w_mix[:, o, :, :], w_sum_sb[:, o, :].unsqueeze(2).broadcast_to([P, C, TAPS]),
                                        w_taps_sb[:, o, :].unsqueeze(1).broadcast_to([P, C, TAPS]), ALU.mult).then_inc(w_mixed, 1)
            dve.wait_ge(ident_ready, 1)
            nc.vector.tensor_reduce(parity[:, :], ident[:, :].rearrange("p (c a q) -> p a c q", c=4, a=2), AX.XY, ALU.add).then_inc(masks_ready, 1)
            nc.vector.tensor_reduce(quarter[:, :], ident[:, :].rearrange("p (c q) -> p c q", c=4), AX.X, ALU.add).then_inc(masks_ready, 1)
            for n in range(4):
                ks = slice(2 * n, 2 * n + 2)
                low(n % 2, n // 2, flat(w_tok_low[:, ks, :]), flat(w_tok_high[:, ks, :]))
            for n in range(3):
                dve.wait_ge(high_done[n % 2], 3 + n // 2)
                weights_qkv(bank[n % 2], [w_qkv_low, w_qkv_high], n, lambda dst, src: nc.vector.tensor_tensor(
                    dst[0], src, dst[1].bitcast(F32), ALU.subtract)).then_inc(copied[n % 2], 1)
            for t in range(TILES):
                take_x(t, 0)
                if t:
                    keep_h(0, t - 1, 0, 0)
            keep_h(0, 3, 0, 0)
            first_variance(0, 0, 0)
            dve.wait_ge(ctl_high_done, 1)
            nc.vector.tensor_tensor(ctl_low[:, :, :], ctl_sb[:, :, :], ctl_high[:, :, :].bitcast(F32), ALU.subtract).then_inc(ctl_split, 1)
            dve.wait_ge(masks_ready, 2)
            dve.wait_ge(vec_loaded, 80)
            nc.vector.tensor_scalar(q_scale[:, :], parity[:, :], HD ** -0.5, None, ALU.mult).then_inc(q_consts, 1)
            dve.wait_ge(q_consts, 1)
            for half in range(2):
                nc.vector.tensor_scalar(q_bias[:, half, :], q_scale[:, :], qkv_bc[:, half:half + 1], None, ALU.mult).then_inc(q_consts, 1)
            first_norm(0)
            take_xn(4)
            for half in range(2):
                keys(0, half, 0, True)
            for t in range(TILES):
                value_rows(t, 2, 2)
            dve.wait_ge(tab_spread, 96)
            with dve.Fori(0, 3) as b:
                j01, j2, j3, jw = jobs_in(b)
                n, j2a, j3a = high_in(b), j2 + 2, j3 + 2
                take_x(0, n)
                row_maxima(b, 0, jw - 1)
                take_x(1, n)
                row_maxima(b, 1, jw - 1)
                keep_h(b + 1, 0, j2, j3)
                take_x(2, n)
                row_maxima(b, 2, jw - 1)
                keep_h(b + 1, 1, j2, j3)
                take_x(3, n)
                row_maxima(b, 3, jw - 1)
                row_sums(b, 0)
                keep_h(b + 1, 2, j2, j3)
                row_sums(b, 1)
                row_sums(b, 2)
                odds(b, 0)
                keep_h(b + 1, 3, j2, j3)
                first_variance(b + 1, j2, j3)
                row_sums(b, 3)
                odds(b, 1)
                turned(0, j2a, j3a)
                first_norm(b + 1)
                odds(b, 2)
                turned(1, j2a, j3a)
                residual(b, 0, j3a)
                odds(b, 3)
                take_xn(n + 4)
                turned(2, j2a, j3a)
                residual(b, 1, j3a)
                turned(3, j2a, j3a)
                keys(b + 1, 0, jw + 1, False)
                residual(b, 2, j3a)
                keys(b + 1, 1, jw + 1, False)
                residual(b, 3, j3a)
                variance(b, stat2, stat2_done, mean_var2, aggr2_done, var_eps2, eps2_added)
                value_rows(0, j2 + 6, j3 + 6)
                value_rows(1, j2 + 6, j3 + 6)
                second_norm(b)
                value_rows(2, j2 + 6, j3 + 6)
                value_rows(3, j2 + 6, j3 + 6)
                route(b, n + 5, j2 + 8)
            for t in range(TILES):
                row_maxima(3, t, 10)
                if t:
                    row_sums(3, t - 1)
            row_sums(3, 3)
            odds(3, 0)
            odds(3, 1)
            turned(0, 31, 28)
            odds(3, 2)
            turned(1, 31, 28)
            residual(3, 0, 28)
            odds(3, 3)
            turned(2, 31, 28)
            residual(3, 1, 28)
            turned(3, 31, 28)
            residual(3, 2, 28)
            residual(3, 3, 28)
            variance(3, stat2, stat2_done, mean_var2, aggr2_done, var_eps2, eps2_added)
            second_norm(3)
            route(3, 23, 35)

            dve.wait_ge(h2_kept, BATCH)
            for t in range(NT):
                k, job = t % 2, t // 2
                dve.wait_ge(x_high_done, t + 1)
                nc.vector.tensor_tensor(x_cur_low[:, t % 4, :], xn2[:, t, :], x_cur_high[:, t % 4, :].bitcast(F32),
                                        ALU.subtract).then_inc(cur_ready, 1)
                dve.wait_ge(filled[k], PREP[k] + END01 + job + 1)
                if t >= 2:
                    dve.wait_ge(filled[5 + 2 * k], ENDW + job)
                nc.vector.tensor_tensor(perm_bd[:, k, :, :], bank[k][:, 0:P].unsqueeze(1).broadcast_to([P, 4, P]),
                                        quarter[:, :].unsqueeze(2).broadcast_to([P, 4, P]), ALU.mult).then_inc(copied[k], 1)
            with dve.Fori(0, 2) as i2:
                for s in range(2):
                    dve.wait_ge(filled[4 + s], ENDW + 8 + i2 + 1)
                    g0 = 8 * (2 * i2 + s)
                    nc.vector.tensor_tensor(innerT[:, bass.ds(g0, ROUND), :], bank[4 + s].rearrange("p (g n) -> p g n", g=ROUND),
                                            f_biasT[:, bass.ds(g0, ROUND)].unsqueeze(2).broadcast_to([P, ROUND, NG]),
                                            ALU.add).then_inc(copied[4 + s], 1)
            for u in (0, 1):
                spread_inner(dve, u, (2, 3), inner_spread_v)
            for u in range(ROUND):
                for i in (1, 3):
                    take_mixed(dve, nc.vector.tensor_copy, u, i)
                if u + 2 < ROUND:
                    spread_inner(dve, u + 2, (2, 3), inner_spread_v)
            def take_turned(s, job):
                k = s % 2
                dve.wait_ge(filled[2 + k], COMB0[2 + k] + job)
                dve.wait_ge(filled[4 * k + 1], COMB0[4 * k + 1] + job + 1)
                nc.vector.tensor_copy(flat(mixed[:, k, 2:4, :]), bank[4 * k + 1][:, :]).then_inc(copied[4 * k + 1], 1)

            def add_experts(s, tile, job, stored):
                k = s % 2
                dve.wait_ge(filled[2 + k], COMB0[2 + k] + job + 1)
                if stored is not None:
                    dve.wait_ge(y_stored[s], stored)
                nc.vector.tensor_tensor(y_sb[:, s, :], bank[2 + k][:, 0:C], tile_of(h, tile), ALU.add).then_inc(copied[2 + k], 1)

            take_turned(0, 0)
            for t in range(4):
                take_turned((t + 1) % 4, (t + 1) // 2)
                add_experts(t, t, t // 2, None)
            with dve.Fori(1, NT // 4 - 1) as i4:
                for s in range(4):
                    take_turned((s + 1) % 4, 2 * i4 + (s + 1) // 2)
                    add_experts(s, 4 * i4 + s, 2 * i4 + s // 2, 16 * i4)
            for t in range(NT - 4, NT):
                if t + 1 < NT:
                    take_turned((t + 1) % 4, (t + 1) // 2)
                add_experts(t % 4, t, t // 2, 16 * (t // 4))

        @block.gpsimd
        def _(pool):
            nc.gpsimd.memset(ident[:, :], 0.0).then_inc(ident_zero, 1)
            pool.wait_ge(ident_zero, 1)
            nc.gpsimd.affine_select(out=ident[:, :], in_=ident[:, :], compare_op=ALU.not_equal, fill=1.0, base=0,
                                    pattern=[[-1, P]], channel_multiplier=1).then_inc(ident_ready, 1)

            def power(b, sem_in, src, dst, sem_out):
                pool.wait_ge(sem_in, b + 1)
                nc.gpsimd.tensor_tensor(dst[:, :], src[:, :], minus_half[:, :], ALU.pow).then_inc(sem_out, 1)

            def add_bias(b):
                for t in range(TILES):
                    nc.gpsimd.tensor_tensor(tile_of(h, 4 * b + t), h1[:, t, :], p_bias[:, :], ALU.add).then_inc(h_biased, 1)

            def shift(b, t):
                pool.wait_ge(max_done, 4 * b + t + 1)
                rows = score[:, t, :, :].rearrange("p n (g r) -> p (n g) r", r=KEYS)
                nc.gpsimd.tensor_tensor(rows, rows, row_max[:, t, :].unsqueeze(2).broadcast_to([P, 16, KEYS]),
                                        ALU.subtract).then_inc(shifted, 1)

            def scale(b, t, jw):
                pool.wait_ge(copied[4 + t], jw + 1)
                pool.wait_ge(inv_done, 4 * b + t + 1)
                rows = att[:, t, :, :].rearrange("p n (m d) -> p (n m) d", d=HD)
                nc.gpsimd.tensor_tensor(rows, rows, row_inv[:, t, :].unsqueeze(2).broadcast_to([P, 16, HD]),
                                        ALU.mult).then_inc(att_scaled, 1)

            def keep(b):
                pool.wait_ge(xn2_ready, 4 * (b + 1))
                nc.gpsimd.tensor_copy(batch_of(xn2, b), xn[:, :, :]).then_inc(xn2_kept, 1)
                nc.gpsimd.tensor_copy(batch_of(h, b), h2[:, :, :]).then_inc(h2_kept, 1)

            pool.wait_ge(copied[0], PREP[0])
            pool.wait_ge(copied[1], PREP[1])
            nc.gpsimd.memset(v_bd[:, :, :, :, :], 0.0).then_inc(bd_zeroed, 1)
            pool.wait_ge(vec_loaded, 80)
            pool.wait_ge(half_set, 1)
            power(0, eps_added, var_eps, rstd, rstd_ready)
            pool.wait_ge(ctl_split, 1)
            pool.wait_ge(tab_loaded, 16)
            nc.gpsimd.memset(k_bd[:, :, :, :], 0.0).then_inc(bd_zeroed, 1)
            add_bias(0)
            with pool.Fori(0, 3) as b:
                j01, j2, j3, jw = jobs_in(b)
                for t in range(TILES):
                    shift(b, t)
                scale(b, 0, jw)
                power(b + 1, eps_added, var_eps, rstd, rstd_ready)
                for t in range(1, TILES):
                    scale(b, t, jw)
                add_bias(b + 1)
                power(b, eps2_added, var_eps2, rstd2, rstd2_ready)
                keep(b)
            for t in range(TILES):
                shift(3, t)
            for t in range(TILES):
                scale(3, t, 11)
            power(3, eps2_added, var_eps2, rstd2, rstd2_ready)
            keep(3)
            pool.wait_ge(perm_done, BATCH)
            pool.wait_ge(xn2_kept, BATCH)
            for t in range(NT):
                if t >= 4:
                    pool.wait_ge(filled[5 + 2 * (t % 2)], ENDW + (t - 4) // 2 + 1)
                nc.gpsimd.tensor_copy(x_cur_high[:, t % 4, :], xn2[:, t, :]).then_inc(x_high_done, 1)
            nc.gpsimd.memset(inner_bd[:, :, :, :, :], 0.0).then_inc(inner_zeroed, 1)


_IN = ["x", "L0_tok_weight", "L0_tok_weighted_sum", "L0_attn_qkv_w", "L0_attn_qkv_b", "L0_attn_rpb", "L0_attn_proj_w",
       "L0_attn_proj_b", "L0_ffn_controller", "L0_ffn_f1", "L0_ffn_bias", "L0_ffn_f2"]


def kernel(**inputs):
    import concourse.bacc as bacc
    from concourse.bass_utils import run_bass_kernel_spmd

    nc = bacc.Bacc("TRN2", target_bir_lowering=False, num_devices=1, dynamic_dma_scratch_size=1024)
    arrays, args = {}, []
    arrays["ties"] = np.float32(1e-6) / np.float32(GROUP - 1) * np.arange(GROUP, dtype=np.float32)
    for name in _IN:
        arrays[name] = np.ascontiguousarray(inputs[name])
        args.append(nc.dram_tensor(name, arrays[name].shape, mybir.dt.from_np(arrays[name].dtype), kind="ExternalInput").ap())
    args.append(nc.dram_tensor("ties", (GROUP,), F32, kind="ExternalInput").ap())
    args.append(nc.dram_tensor("out", (BATCH, SEQ, C), F32, kind="ExternalOutput").ap())
    build(nc, *args)
    r = run_bass_kernel_spmd(nc, [arrays], core_ids=[0])
    return r.results[0]["out"]
```

```python
from contextlib import ExitStack

import numpy as np

import concourse.bass as bass
from concourse import mybir

F32 = mybir.dt.float32
F32R = mybir.dt.float32r
ALU = mybir.AluOpType
ACT = mybir.ActivationFunctionType
AX = mybir.AxisListType

P = 128
BATCH, SEQ, C, TAPS = 4, 512, 256, 4
TILES = SEQ // P
NT = BATCH * TILES
KIN = C * TAPS
HD, WIN = 16, 13
RPB = 2 * WIN - 1
BLK = 16
KEYS = 32
NBLK = SEQ // BLK
MASKED = -1.0e38
EPS = 1e-5
GROUP = 32
NG = BATCH * SEQ // GROUP
EXPERTS, FF = 128, 32
ROUND = 8

PREP = (3, 2)
HIGH0 = (2, 1)
X0 = (0, 0)
WIDE0 = 1
SBUF_FROM, SBUF_TO = 2 * 1024, 229344


def key_base(blk):
    return min(max(BLK * blk - 8, 0), SEQ - KEYS)


def neighbourhood(blk, q):
    query = BLK * blk + q
    first = min(max(query - WIN // 2, 0), SEQ - WIN)
    return first - key_base(blk), first - query + WIN - 1


def build(nc, x, w_taps, w_sum, qkv_w, qkv_b, rpb, proj_w, proj_b, controller, f1, f_bias, f2, ties, out):
    x_d = x.rearrange("b (t p) i d -> (b t) p (i d)", p=P)
    out_d = out.rearrange("b (t p) c -> (b t) p c", p=P)
    f1_d = f1.rearrange("(k p) e s f -> p k (e s f)", p=P)
    f2_d = f2.rearrange("e s f d -> (e s f) d")
    v_scratch = nc.dram_tensor("v_scratch", [SEQ, C], F32, kind="Internal").ap()
    tab_scratch = nc.dram_tensor("tab_scratch", [3, 2, BLK, 8, KEYS], F32, kind="Internal").ap()

    with ExitStack() as ctx:
        ctx.enter_context(nc.allow_non_contiguous_dma(reason="small weights and windows"))

        def sem(name):
            return ctx.enter_context(nc.semaphore(name))

        bank = [ctx.enter_context(nc.psum_tensor(f"bank{i}", [P, 512], F32)) for i in range(8)]

        at = [SBUF_FROM]

        def place(name, *shape, dt=F32):
            tensor = nc.alloc_sbuf_tensor_at(name, [P, *shape], dt, offset=at[0])
            at[0] += (4 * int(np.prod(shape)) + 31) // 32 * 32
            assert at[0] <= SBUF_TO, (name, at[0])
            return tensor

        ident = place("ident", P)
        parity = place("parity", 2)
        quarter = place("quarter", 4)
        h = place("h", NT, C)
        xn2_from = at[0]
        xn2 = place("xn2", NT, C)
        permT = place("permT", NT * P)
        f_biasT = place("f_biasT", 32)
        phase_start = at[0]

        x_sb = place("x_sb", TILES, KIN)
        xT_high, xT_low = (place(f"xT_{n}", 2, 8, P, dt=F32R) for n in ("high", "low"))
        w_tok_high, w_tok_low = (place(f"w_tok_{n}", 8, C, dt=F32R) for n in ("high", "low"))
        w_qkv_high, w_qkv_low = (place(f"w_qkv_{n}", 2, 3 * C, dt=F32R) for n in ("high", "low"))
        q_eo = place("q_eo", 2, NBLK, 2, BLK)
        kT = place("kT", 2, SEQ)
        k_bd_from = at[0]
        k_bd = place("k_bd", 2, 4, SEQ)
        v_sb = place("v_sb", TILES, C)
        v_bd_from = at[0]
        v_bd = place("v_bd", NBLK, 4, 2, 32)
        v_bd_end = at[0]
        ctl_high, ctl_low = (place(f"ctl_{n}", 2, EXPERTS, dt=F32R) for n in ("high", "low"))
        xnT_high, xnT_low = (place(f"xnT_{n}", 2, SEQ, dt=F32R) for n in ("high", "low"))
        w_proj = place("w_proj", 2, C)
        h1 = place("h1", TILES, C)
        h2 = place("h2", TILES, C)
        xn = place("xn", TILES, C)
        score = place("score", TILES, 4, P)
        probT = place("probT", 2, 4, P)
        even = place("even", 2, 256)
        att = place("att", TILES, 2, P)
        attT = place("attT", 2, 2, P)
        logit = place("logit", SEQ)
        bias_tab = place("bias_tab", 4, 256)
        v_bias = place("v_bias", C)
        p_bias = place("p_bias", C)
        tie = place("tie", GROUP)
        row_max, row_sum, row_inv = (place(f"row_{n}", TILES, 16) for n in ("max", "sum", "inv"))
        stat, stat2 = (place(n, TILES, 6) for n in ("stat", "stat2"))
        mean_var, mean_var2 = (place(n, TILES, 2) for n in ("mean_var", "mean_var2"))
        var_eps, var_eps2, rstd, rstd2, minus_half = (place(n, TILES) for n in ("var_eps", "var_eps2", "rstd", "rstd2", "minus_half"))
        qkv_bc = place("qkv_bc", 4)
        q_scale = place("q_scale", 2)
        q_bias = place("q_bias", 2, 2)
        gmax = place("gmax", SEQ // GROUP)

        at[0] = k_bd_from
        w_sum_sb = place("w_sum_sb", 2, C)
        w_taps_sb = place("w_taps_sb", 2, TAPS)
        ctl_sb = place("ctl_sb", 2, EXPERTS)
        tab_fill = place("tab_fill", 256)
        at[0] = v_bd_from
        w_mix = place("w_mix", 2, C, TAPS)
        qkv_sb = place("qkv_sb", 6, C)
        proj_sb = place("proj_sb", 2, C)
        f_bias_sb = place("f_bias_sb", P)

        at[0] = phase_start
        f1_early = place("f1_early", 2, 2, 4, ROUND * FF)
        dispT_from = at[0]
        dispT = place("dispT", 2, EXPERTS, NG)
        x_cur_from = at[0]
        x_cur_high, x_cur_low = (place(f"x_cur_{n}", 4, C, dt=F32R) for n in ("high", "low"))
        perm_bd = place("perm_bd", 2, 4, P, dt=F32R)
        assert at[0] <= v_bd_from
        at[0] = dispT_from
        interT = place("interT", 2, NG, EXPERTS)
        at[0] = v_bd_from
        f2_sb = place("f2_sb", 32, C)
        assert at[0] <= v_bd_end
        at[0] = v_bd_from
        f2_low = place("f2_low", 32, C, dt=F32R)
        f1_late = place("f1_late", 2, 2, 4, ROUND * FF)
        innerT = place("innerT", 32, NG)
        inner_high = place("inner_high", 2, 4, 4, NG, dt=F32R)
        mixed = place("mixed", 2, 4, C)
        y_sb = place("y_sb", 4, C)
        at[0] = xn2_from
        f2_high_a = place("f2_high_a", 16, C, dt=F32R)
        at[0] = phase_start
        f2_high_b = place("f2_high_b", 16, C, dt=F32R)
        at[0] = x_cur_from
        inner_low = place("inner_low", 2, 4, 4, NG, dt=F32R)

        filled = [sem(f"filled{i}") for i in range(8)]
        copied = [sem(f"copied{i}") for i in range(8)]
        x_loaded = [sem(f"x_loaded{i}") for i in range(TILES)]
        ident_zero, ident_ready, masks_ready = sem("ident_zero"), sem("ident_ready"), sem("masks_ready")
        tok_w_loaded, qkv_w_loaded, vec_loaded = sem("tok_w_loaded"), sem("qkv_w_loaded"), sem("vec_loaded")
        ctl_loaded = sem("ctl_loaded")
        w_mixed, q_consts = sem("w_mixed"), sem("q_consts")
        w_high_done = sem("w_high_done")
        high_done = [sem(f"high_done{i}") for i in range(2)]
        ctl_high_done, ctl_split = sem("ctl_high_done"), sem("ctl_split")
        x_high_done = sem("x_high_done")
        tab_masked, tab_loaded, tab_spread = sem("tab_masked"), sem("tab_loaded"), sem("tab_spread")
        bd_zeroed, half_set = sem("bd_zeroed"), sem("half_set")
        stat_done, aggr_done, eps_added, rstd_ready = (sem(n) for n in ("stat_done", "aggr_done", "eps_added", "rstd_ready"))
        xn_ready, h_biased = sem("xn_ready"), sem("h_biased")
        k_spread, v_written, v_spread = sem("k_spread"), sem("v_written"), sem("v_spread")
        max_done, shifted, exp_done, sum_done, inv_done = (sem(n) for n in ("max_done", "shifted", "exp_done", "sum_done", "inv_done"))
        even_done, att_scaled = sem("even_done"), sem("att_scaled")
        h2_kept, stat2_done, aggr2_done, eps2_added, rstd2_ready = (sem(n) for n in ("h2_kept", "stat2_done", "aggr2_done", "eps2_added", "rstd2_ready"))
        xn2_ready, xn2_kept = sem("xn2_ready"), sem("xn2_kept")
        gmax_done, perm_done = sem("gmax_done"), sem("perm_done")
        cur_ready = sem("cur_ready")
        f1_loaded = [sem(f"f1_loaded{i}") for i in range(4)]
        f2_loaded = sem("f2_loaded")
        inner_zeroed, inner_high_done, inner_split = sem("inner_zeroed"), sem("inner_high_done"), sem("inner_split")
        f2_high_done, f2_split_v, f2_split_p = sem("f2_high_done"), sem("f2_split_v"), sem("f2_split_p")
        y_stored = [sem(f"y_stored{i}") for i in range(4)]

        block = ctx.enter_context(nc.Block())

        def jobs_in(b):
            return 5 + 8 * b, 4 + 9 * b, 4 + 8 * b, WIDE0 + 2 + 3 * b

        def high_in(b):
            return 5 + 6 * b

        def after(base, n):
            return base[0] + n, base[1] + n

        L01, L2, L3, LW = jobs_in(BATCH - 1)
        END01, END2, END3, ENDW = L01 + 3, L2 + 5, L3 + 4, LW + 1
        XN_TURNED = L01 + 4

        def perm_job(t):
            return PREP[t % 2] + L01 + 2 + t // 2 + (1 if t >= 4 else 0)

        MIX0 = [PREP[0] + END01 + 8, PREP[1] + END01 + 8, END2, END3] + [ENDW + 8 + 2, ENDW + 8 + 2, ENDW + 8, ENDW + 8]
        COMB0 = [n + 4 for n in MIX0]

        @block.sync
        def _(sp):
            def load_x(b, waits):
                for t in range(TILES):
                    if waits is not None:
                        sp.wait_ge(copied[1], waits + t + 1)
                    sp.dma_start(x_sb[:, t, :], x_d[4 * b + t, :, :] if isinstance(b, int) else
                                 x_d[bass.ds(4 * b + t, 1), :, :].rearrange("a p n -> (a p) n")).then_inc(x_loaded[t], 16)

            def spread_kv(b, jw, j3, first):
                for i in (6, 7):
                    sp.wait_ge(copied[i], jw + 1)
                for g in range(4):
                    sp.dma_start(k_bd[32 * g:32 * g + 32, :, g, :], kT[32 * g:32 * g + 32, :, :]).then_inc(k_spread, 16)
                sp.wait_ge(copied[3], j3)
                if not first:
                    sp.wait_ge(v_spread, 128 * b)
                sp.dma_start(v_scratch.rearrange("(t p) c -> p t c", p=P), v_sb[:, :, :]).then_inc(v_written, 16)
                sp.wait_ge(v_written, 16 * (b + 1))
                for g in range(4):
                    rows = slice(32 * g, 32 * g + 32)
                    inner = bass.AP(v_scratch.tensor, (BLK - 8) * C + 64 * g, [[C, KEYS], [BLK * C, NBLK - 2], [1, 64]])
                    edges = bass.AP(v_scratch.tensor, 64 * g, [[C, KEYS], [(SEQ - KEYS) * C, 2], [1, 64]])
                    v4 = v_bd[rows, :, g, :, :].rearrange("p n a c -> p n (a c)")
                    sp.dma_start(v4[:, 1:NBLK - 1, :], inner).then_inc(v_spread, 16)
                    sp.dma_start(v4[:, 0:NBLK:NBLK - 1, :], edges).then_inc(v_spread, 16)

            sp.dma_start(w_sum_sb[:, :, :], w_sum.rearrange("(o p) i -> p o i", p=P)).then_inc(tok_w_loaded, 16)
            sp.dma_start(w_taps_sb[:, :, :], w_taps.rearrange("(o p) d -> p o d", p=P)).then_inc(tok_w_loaded, 16)
            load_x(0, None)
            sp.dma_start(qkv_sb[:, :, :], qkv_w.rearrange("(r p) c -> p r c", p=P)).then_inc(qkv_w_loaded, 16)
            for r in range(2):
                for a in range(2):
                    sp.dma_start(proj_sb[:, r, a * P:(a + 1) * P].rearrange("p (n d) -> p n d", d=HD),
                                 proj_w[r * P:(r + 1) * P, :].rearrange("p (n a d) -> p a n d", a=2, d=HD)[:, a, :, :]).then_inc(qkv_w_loaded, 16)
            sp.dma_start(f_bias_sb[0:32, :].rearrange("g (j f) -> g j f", j=4),
                         f_bias.rearrange("e s f -> (e s f)").rearrange("(j g f) -> g j f", j=4, g=32)).then_inc(qkv_w_loaded, 16)
            sp.wait_ge(tab_masked, 1)
            sp.dma_start(tab_scratch.rearrange("v a q n r -> (v a q) (n r)"), tab_fill[0:96, :]).then_inc(tab_loaded, 16)
            sp.dma_start(ctl_sb[:, :, :], controller.rearrange("(k p) e s -> p k (e s)", p=P)).then_inc(ctl_loaded, 16)
            sp.dma_start(qkv_bc[:, :], qkv_b.rearrange("(r p) -> p r", p=P)[:, 0:4]).then_inc(vec_loaded, 16)
            for a in range(2):
                sp.dma_start(v_bias[:, :].rearrange("p (g a c) -> p a g c", g=4, a=2)[:, a, :, :],
                             bass.AP(qkv_b.tensor, 2 * C + 128 * a, [[0, P], [32, 4], [1, 32]])).then_inc(vec_loaded, 16)
            sp.dma_start(p_bias[:, :], bass.AP(proj_b.tensor, 0, [[0, P], [1, C]])).then_inc(vec_loaded, 16)
            sp.dma_start(tie[:, :], bass.AP(ties.tensor, 0, [[0, P], [1, GROUP]])).then_inc(vec_loaded, 16)
            sp.wait_ge(tab_loaded, 16)
            runs = 0
            for v, blk in enumerate((0, 1, NBLK - 1)):
                q = 0
                while q < BLK:
                    (r0, s0), n = neighbourhood(blk, q), 1
                    while q + n < BLK and neighbourhood(blk, q + n) == (r0 + n, s0):
                        n += 1
                    row = (v * 2 * BLK + q) * 256 + r0
                    if n == 1:
                        pairs = [(bass.AP(tab_scratch.tensor, row, [[BLK * 256, 2], [KEYS, 8], [1, WIN]]),
                                  bass.AP(rpb.tensor, s0, [[RPB, 2], [2 * RPB, 8], [1, WIN]]))]
                    else:
                        pairs = [(bass.AP(tab_scratch.tensor, row + par * BLK * 256, [[256 + 1, n], [KEYS, 8], [1, WIN]]),
                                  bass.AP(rpb.tensor, par * RPB + s0, [[0, n], [2 * RPB, 8], [1, WIN]])) for par in range(2)]
                    for dst, src in pairs:
                        sp.dma_start(dst, src).then_inc(tab_loaded, 16)
                        runs += 1
                    q += n
            sp.wait_ge(tab_loaded, 16 * (1 + runs))
            for quad in range(4):
                sp.dma_start(bias_tab[:, quad, :], bass.AP(tab_scratch.tensor, 32 * 256, [[0, 4], [256, 32], [1, 256]])).then_inc(tab_spread, 16)
            sp.wait_ge(tab_spread, 64)
            sp.dma_start(bias_tab[0:32, 0, :], bass.AP(tab_scratch.tensor, 0, [[256, 32], [1, 256]])).then_inc(tab_spread, 16)
            sp.dma_start(bias_tab[96:128, 3, :], bass.AP(tab_scratch.tensor, 2 * 32 * 256, [[256, 32], [1, 256]])).then_inc(tab_spread, 16)
            load_x(1, X0[1])
            sp.wait_ge(bd_zeroed, 2)
            spread_kv(0, WIDE0, 4, True)
            with sp.Fori(0, 2) as b:
                j01, j2, j3, jw = jobs_in(b)
                load_x(b + 2, PREP[1] + j01)
                spread_kv(b + 1, jw + 1, j3 + 8, False)
            j01, j2, j3, jw = jobs_in(2)
            sp.wait_ge(filled[2], j2 + 2)
            sp.wait_ge(filled[3], j3 + 2)

            def load_f1(f1_sb, rounds):
                for rnd in rounds:
                    for k in range(2):
                        sp.dma_start(f1_sb[:, rnd % 2, k, :, :], f1_d.rearrange("p k (j g n) -> p k j g n", j=4, g=4)
                                     [:, k, :, rnd, :]).then_inc(f1_loaded[rnd], 16)

            load_f1(f1_early, (0, 1))
            spread_kv(3, jw + 1, j3 + 8, False)
            sp.wait_ge(filled[7], ENDW)
            for j in range(4):
                sp.dma_start(f2_sb[32 * j:32 * j + 32, :, :],
                             f2_d.rearrange("(j g f) d -> j f g d", j=4, g=32)[j]).then_inc(f2_loaded, 16)
            sp.wait_ge(perm_done, BATCH)
            sp.wait_ge(h2_kept, BATCH - 1)
            load_f1(f1_late, (2, 3))
            for t in range(NT):
                sp.wait_ge(copied[2 + t % 2], COMB0[2 + t % 2] + t // 2 + 1)
                sp.dma_start(out_d[t], y_sb[:, t % 4, :]).then_inc(y_stored[t % 4], 16)
            for s in range(4):
                sp.wait_ge(y_stored[s], 16 * (NT // 4))

        @block.tensor
        def _(pe):
            def room(i, job):
                if not (isinstance(job, int) and job == 0):
                    pe.wait_ge(copied[i], job)

            def turn4(i, job, sources):
                room(i, job)
                n = 0
                for s in sources:
                    k, m = s.shape[0], int(np.prod(s.shape[1:]))
                    last = nc.tensor.transpose(bank[i][0:m, n:n + k], s, ident[0:k, 0:k])
                    n += k
                last.then_inc(filled[i], 1)

            def products(out, terms):
                passes = [(lh, rh) for lh, ll, rh, rl in terms] + [(lh, rl) for lh, ll, rh, rl in terms] + \
                         [(ll, rh) for lh, ll, rh, rl in terms]
                for n, (lhs, rhs) in enumerate(passes):
                    last = nc.tensor.matmul(out, lhs, rhs, start=(n == 0), stop=(n == len(passes) - 1))
                return last

            def turn_token_weights():
                pe.wait_ge(ident_ready, 1)
                for n in range(4):
                    pe.wait_ge(w_mixed, 2 * (n + 1))
                    turn4(4 + n, 0, [w_mix[:, :, :, :].rearrange("p o i d -> p o (i d)")[:, o, k * P:(k + 1) * P]
                                          for k in (2 * n, 2 * n + 1) for o in range(2)])

            def turn_qkv_weights(n):
                pe.wait_ge(qkv_w_loaded, 96)
                turn4(n % 2, X0[n % 2] + TILES + n // 2, [qkv_sb[:, r, k * P:(k + 1) * P] for r in (2 * n, 2 * n + 1) for k in range(2)])

            def turn_x(b, t, base):
                pe.wait_ge(x_loaded[t], 16 * (b + 1))
                for i in range(2):
                    turn4(i, base[i] + t, [x_sb[:, t, (4 * i + k) * P:(4 * i + k + 1) * P] for k in range(4)])

            def token_products(t, base, j2, j3):
                i, j = (2, j2) if t % 2 == 0 else (3, j3)
                pe.wait_ge(copied[0], base[0] + t + 1)
                pe.wait_ge(copied[1], base[1] + t + 1)
                room(i, j + t // 2)
                s = t % 2
                products(bank[i][:, 0:C], [(xT_high[:, s, k, :], xT_low[:, s, k, :], w_tok_high[:, k, :], w_tok_low[:, k, :])
                                           for k in range(8)]).then_inc(filled[i], 1)

            def turn_xn(b, j01, ready, rows=xn, first=0):
                pe.wait_ge(ready, 4 * (b + 1))
                for i in range(2):
                    turn4(i, PREP[i] + j01, [rows[:, first + t, i * P:(i + 1) * P] for t in range(TILES)])

            def wide(r, j01, jw):
                if r == 2:
                    for i in range(2):
                        pe.wait_ge(copied[i], PREP[i] + j01 + 1)
                room(4 + r, jw)
                products(bank[4 + r][:, :], [(w_qkv_high[:, k, r * P:(r + 1) * P], w_qkv_low[:, k, r * P:(r + 1) * P],
                                              xnT_high[:, k, :], xnT_low[:, k, :]) for k in range(2)]).then_inc(filled[4 + r], 1)

            def value_rows(t, j2, j3):
                i, j = (2, j2) if t % 2 == 0 else (3, j3)
                room(i, j + t // 2)
                products(bank[i][:, 0:C], [(xnT_high[:, k, t * P:(t + 1) * P], xnT_low[:, k, t * P:(t + 1) * P],
                                            w_qkv_high[:, k, 2 * C:3 * C], w_qkv_low[:, k, 2 * C:3 * C])
                                           for k in range(2)]).then_inc(filled[i], 1)

            def scores(b, jw, tiles):
                if 0 in tiles:
                    pe.wait_ge(k_spread, 64 * (b + 1))
                    for i in (4, 5):
                        pe.wait_ge(copied[i], jw)
                for t in tiles:
                    room(4 + t, jw)
                    for n in range(4):
                        for c in range(4):
                            blk, half = 8 * t + 4 * (n // 2) + c, n % 2
                            last = nc.tensor.matmul(bank[4 + t][32 * c:32 * c + 32, n * P:(n + 1) * P],
                                                    q_eo[:, half, blk, :, :].rearrange("p a q -> p (a q)"),
                                                    k_bd[:, half, :, key_base(blk):key_base(blk) + KEYS],
                                                    start=True, stop=True, tile_position=(0, 32 * c))
                    last.then_inc(filled[4 + t], 1)

            def turn_probs(b, t, j01):
                pe.wait_ge(exp_done, 4 * b + t + 1)
                turn4(t % 2, PREP[t % 2] + j01 + t // 2, [score[:, t, n, :] for n in range(4)])

            def values(b, t, j01, jw):
                pe.wait_ge(copied[t % 2], PREP[t % 2] + j01 + t // 2 + 1)
                if t == 0:
                    pe.wait_ge(v_spread, 128 * (b + 1))
                room(4 + t, jw)
                for n in range(4):
                    for c in range(4):
                        blk, half = 8 * t + 4 * (n // 2) + c, n % 2
                        last = nc.tensor.matmul(bank[4 + t][32 * c:32 * c + 32, n * P:(n + 1) * P],
                                                probT[:, t % 2, n, 32 * c:32 * c + 32], v_bd[:, blk, :, half, :],
                                                start=True, stop=True, tile_position=(0, 32 * c))
                last.then_inc(filled[4 + t], 1)

            def turn_att(b, t, j2):
                pe.wait_ge(att_scaled, 4 * b + t + 1)
                turn4(2, j2 + t, [att[:, t, n, :] for n in range(2)])

            def out_proj(t, j2, j3):
                pe.wait_ge(copied[2], j2 + t + 1)
                room(3, j3 + t)
                for a in range(2):
                    last = nc.tensor.matmul(bank[3][:, 0:C], attT[:, t % 2, a, :], w_proj[:, a, :], start=(a == 0), stop=(a == 1))
                last.then_inc(filled[3], 1)

            def route(b, j01, j2):
                for i in range(2):
                    pe.wait_ge(copied[i], PREP[i] + j01 + 1)
                room(2, j2)
                products(bank[2][:, :], [(ctl_high[:, k, :], ctl_low[:, k, :], xnT_high[:, k, :], xnT_low[:, k, :])
                                         for k in range(2)]).then_inc(filled[2], 1)

            turn_token_weights()
            turn_x(0, 0, X0)
            turn_x(0, 1, X0)
            for i in range(4, 8):
                pe.wait_ge(copied[i], WIDE0)
            token_products(0, X0, 0, 0)
            turn_x(0, 2, X0)
            token_products(1, X0, 0, 0)
            turn_x(0, 3, X0)
            token_products(2, X0, 0, 0)
            turn_qkv_weights(0)
            turn_qkv_weights(1)
            token_products(3, X0, 0, 0)
            turn_qkv_weights(2)
            turn4(1, PREP[1] + 3, [proj_sb[:, o, a * P:(a + 1) * P] for a in range(2) for o in range(2)])
            turn4(0, PREP[0] + 3, [f_bias_sb[0:32, :]])
            turn_xn(0, 4, xn_ready)
            for r in (2, 3, 0, 1):
                wide(r, 4, WIDE0)
            for t in range(TILES):
                value_rows(t, 2, 2)
            scores(0, WIDE0 + 1, (0, 1, 2))
            with pe.Fori(0, 3) as b:
                j01, j2, j3, jw = jobs_in(b)
                ja, j2a, j3a = j01 + 4, j2 + 2, j3 + 2
                x_jobs = after(PREP, j01)
                turn_x(b + 1, 0, x_jobs)
                scores(b, jw - 1, (3,))
                turn_x(b + 1, 1, x_jobs)
                token_products(0, x_jobs, j2, j3)
                turn_x(b + 1, 2, x_jobs)
                token_products(1, x_jobs, j2, j3)
                turn_x(b + 1, 3, x_jobs)
                token_products(2, x_jobs, j2, j3)
                turn_probs(b, 0, ja)
                turn_probs(b, 1, ja)
                token_products(3, x_jobs, j2, j3)
                values(b, 0, ja, jw)
                turn_probs(b, 2, ja)
                values(b, 1, ja, jw)
                turn_probs(b, 3, ja)
                turn_att(b, 0, j2a)
                values(b, 2, ja, jw)
                out_proj(0, j2a, j3a)
                turn_att(b, 1, j2a)
                values(b, 3, ja, jw)
                turn_xn(b + 1, ja + 2, xn_ready)
                turn_att(b, 2, j2a)
                out_proj(1, j2a, j3a)
                wide(2, ja + 2, jw + 1)
                turn_att(b, 3, j2a)
                out_proj(2, j2a, j3a)
                wide(3, ja + 2, jw + 1)
                out_proj(3, j2a, j3a)
                wide(0, ja + 2, jw + 1)
                wide(1, ja + 2, jw + 1)
                for t in range(TILES):
                    value_rows(t, j2 + 6, j3 + 6)
                turn_xn(b, ja + 3, xn2_ready)
                scores(b + 1, jw + 2, (0, 1,))
                route(b, ja + 3, j2 + 8)
                scores(b + 1, jw + 2, (2,))
            scores(3, LW - 1, (3,))
            turn_probs(3, 0, L01)
            turn_probs(3, 1, L01)
            values(3, 0, L01, LW)
            turn_probs(3, 2, L01)
            values(3, 1, L01, LW)
            turn_att(3, 0, L2)
            turn_probs(3, 3, L01)
            values(3, 2, L01, LW)
            turn_att(3, 1, L2)
            out_proj(0, L2, L3)
            values(3, 3, L01, LW)
            turn_att(3, 2, L2)
            out_proj(1, L2, L3)

            def turn_perm(t):
                if t % TILES == 0:
                    pe.wait_ge(perm_done, t // TILES + 1)
                turn4(t % 2, perm_job(t), [permT[:, t * P:(t + 1) * P]])

            def dispatch(t):
                pe.wait_ge(copied[t % 2], perm_job(t) + 1)
                pe.wait_ge(cur_ready, t + 1)
                for half in range(2):
                    k = 4 + 2 * (t % 2) + half
                    room(k, ENDW + t // 2)
                    cols = slice(half * P, (half + 1) * P)
                    nc.tensor.matmul(bank[k][:, :], x_cur_high[:, t % 4, cols], perm_bd[:, t % 2, :, :], start=True, stop=False)
                    nc.tensor.matmul(bank[k][:, :], x_cur_low[:, t % 4, cols], perm_bd[:, t % 2, :, :],
                                     start=False, stop=True).then_inc(filled[k], 1)

            turn_perm(0)
            turn_att(3, 3, L2)
            out_proj(2, L2, L3)
            turn_perm(1)
            out_proj(3, L2, L3)
            dispatch(0)
            turn_perm(2)
            dispatch(1)
            turn_perm(3)
            dispatch(2)
            turn_xn(3, XN_TURNED, xn2_ready, xn2, NT - TILES)
            dispatch(3)
            turn_perm(4)
            route(3, XN_TURNED, L2 + 4)
            for t in range(4, NT):
                if t + 1 < NT:
                    turn_perm(t + 1)
                dispatch(t)
            for k in range(4, 8):
                pe.wait_ge(copied[k], ENDW + 8)
            for rnd in range(4):
                s = rnd % 2
                pe.wait_ge(f1_loaded[rnd], 32)
                room(4 + s, ENDW + 8 + rnd // 2)
                for g in range(ROUND):
                    for k in range(2):
                        for j in range(4):
                            last = nc.tensor.matmul(bank[4 + s][32 * j:32 * j + 32, g * NG:(g + 1) * NG],
                                                    (f1_early, f1_late)[rnd // 2][:, s, k, j, g * FF:(g + 1) * FF],
                                                    dispT[:, k, 32 * j + 8 * rnd + g, :],
                                                    start=(k == 0), stop=(k == 1), tile_position=(0, 32 * j))
                last.then_inc(filled[4 + s], 1)
            for u in range(ROUND):
                if u % 2 == 0:
                    pe.wait_ge((f2_split_v, f2_split_p)[u // 4], u // 2 % 2 + 1)
                pe.wait_ge(inner_split, 4 * (u + 1))
                for i in range(4):
                    s, q = 4 * (u % 2) + i, 4 * u + i
                    f2_high = f2_high_a if q < 16 else f2_high_b
                    room(s, MIX0[s] + u // 2)
                    for half in range(2):
                        cols = slice(half * P, (half + 1) * P)
                        last = products(bank[s][:, half * C:(half + 1) * C],
                                        [(f2_high[:, q % 16, cols], f2_low[:, q, cols],
                                          inner_high[:, u % 2, i, :, :], inner_low[:, u % 2, i, :, :])])
                    last.then_inc(filled[s], 1)
            def turn_mixed(t):
                for a in range(2):
                    i = 4 * (t % 2) + a
                    turn4(i, COMB0[i] + t // 2, [interT[:, half, 4 * t + c, :] for c in (2 * a, 2 * a + 1) for half in range(2)])

            for s in range(8):
                pe.wait_ge(copied[s], COMB0[s])
            turn_mixed(0)
            for t in range(NT):
                if t + 1 < NT:
                    turn_mixed(t + 1)
                for a in range(2):
                    pe.wait_ge(copied[4 * (t % 2) + a], COMB0[4 * (t % 2) + a] + t // 2 + 1)
                room(2 + t % 2, COMB0[2 + t % 2] + t // 2)
                for c in range(4):
                    last = nc.tensor.matmul(bank[2 + t % 2][32 * c:32 * c + 32, 0:C], permT[:, (4 * t + c) * 32:(4 * t + c + 1) * 32],
                                            mixed[:, t % 2, c, :], start=True, stop=True, tile_position=(0, 32 * c))
                last.then_inc(filled[2 + t % 2], 1)

        def weights_qkv(src, parts, n, put):
            view = src.rearrange("p (r k o) -> p r k o", r=2, k=2)
            for r in range(2):
                if n < 2:
                    pick = [w[:, :, (2 * n + r) * P:(2 * n + r + 1) * P] for w in parts]
                    last = put(pick, view[:, r, :, :])
                else:
                    pick = [w[:, :, 2 * C:3 * C].rearrange("p k (g a c) -> p a k g c", g=4, a=2)[:, r, :, :, :] for w in parts]
                    last = put(pick, view[:, r, :, :].rearrange("p k (g c) -> p k g c", g=4))
            return last

        def inner_slot_free(eng, u):
            if u == 0:
                eng.wait_ge(inner_zeroed, 2)
            if u >= 2:
                for s in range(4 * (u % 2), 4 * (u % 2) + 4):
                    eng.wait_ge(filled[s], MIX0[s] + (u - 2) // 2 + 1)

        def f2_lows(eng, ops, n, done):
            qs = slice(8 * n, 8 * n + 8)
            high_part = (f2_high_a, f2_high_b)[n // 2][:, 8 * (n % 2):8 * (n % 2) + 8, :]
            eng.wait_ge(f2_high_done, n + 1)
            ops.tensor_tensor(f2_low[:, qs, :], f2_sb[:, qs, :], high_part.bitcast(F32), ALU.subtract).then_inc(done, 1)

        def diagonal(u, j):
            return slice(32 * j, 32 * j + 32), (slice(32 * j, 32 * j + 32), u % 2, slice(None), j, slice(None))

        def take_mixed(eng, copy, u, i):
            s = 4 * (u % 2) + i
            eng.wait_ge(filled[s], MIX0[s] + u // 2 + 1)
            dst = interT[:, :, :, 4 * u + i:EXPERTS:32].rearrange("p a g j -> p a j g")
            src = bank[s].rearrange("p (a j g) -> p a j g", a=2, j=4)
            copy(dst, src).then_inc(copied[s], 1)

        def batch_of(tensor, b):
            return tensor[:, bass.ds(4 * b, 4), :]

        def tile_of(tensor, n):
            return tensor[:, bass.ds(n, 1), :].rearrange("p a c -> p (a c)")

        def flat(ap):
            return ap.rearrange("p a b -> p (a b)")

        @block.scalar
        def _(act):
            def take(i, job, dst, src):
                act.wait_ge(filled[i], job + 1)
                nc.scalar.copy(dst, src).then_inc(copied[i], 1)

            def high(i, job, dst, done=None):
                act.wait_ge(filled[i], job + 1)
                nc.scalar.copy(dst, bank[i][:, :]).then_inc(high_done[i] if done is None else done, 1)

            def take_x(t, base, j2, j3):
                if t >= 2:
                    act.wait_ge(filled[2 + t % 2], (j2, j3)[t % 2] + 1)
                for i in range(2):
                    high(i, base[i] + t, flat(xT_high[:, t % 2, 4 * i:4 * i + 4, :]))

            def exps(b, t):
                act.wait_ge(shifted, 4 * b + t + 1)
                nc.scalar.activation(score[:, t, :, :], score[:, t, :, :], ACT.Exp).then_inc(exp_done, 1)

            def take_xn(j01):
                for i in range(2):
                    high(i, PREP[i] + j01, xnT_high[:, i, :])

            def keep_h(b, t):
                i = 2 + t % 2
                if t == 0 and not (isinstance(b, int) and b == 0):
                    act.wait_ge(h_biased, 4 * b)
                act.wait_ge(stat_done, 4 * b + t + 1)
                nc.scalar.copy(h1[:, t, :], bank[i][:, 0:C]).then_inc(copied[i], 1)

            def keys(b, half, jw, first):
                if half == 0 and not first:
                    act.wait_ge(k_spread, 64 * b)
                act.wait_ge(filled[6 + half], jw + 1)
                nc.scalar.activation(kT[:, half, :], bank[6 + half][:, :], ACT.Identity,
                                     bias=qkv_bc[:, 2 + half:3 + half]).then_inc(copied[6 + half], 1)

            def queries(half, jw):
                act.wait_ge(filled[4 + half], jw + 1)
                for a in range(2):
                    last = nc.scalar.activation(q_eo[:, half, :, a, :], bank[4 + half].rearrange("p (n q) -> p n q", q=BLK), ACT.Identity,
                                                bias=q_bias[:, half, a:a + 1], scale=q_scale[:, a:a + 1])
                last.then_inc(copied[4 + half], 1)

            def probs(t, j01, jw):
                if t >= 2:
                    act.wait_ge(filled[4 + t - 2], jw + 1)
                take(t % 2, PREP[t % 2] + j01 + t // 2, flat(probT[:, t % 2, :, :]), bank[t % 2][:, :])

            def evens(t, jw):
                act.wait_ge(filled[4 + t], jw + 1)
                if t >= 2:
                    act.wait_ge(copied[4 + t - 2], jw + 1)
                nc.scalar.mul(even[:, t % 2, :].rearrange("p (n d) -> p n d", d=HD),
                              bank[4 + t].rearrange("p (n a d) -> p n a d", a=2, d=HD)[:, :, 0, :],
                              parity[:, 0:1]).then_inc(even_done, 1)

            for n in range(4):
                high(4 + n, 0, flat(w_tok_high[:, 2 * n:2 * n + 2, :]), w_high_done)
            for t in range(TILES):
                take_x(t, X0, 0, 0)
                if t:
                    keep_h(0, t - 1)
            for n in range(3):
                if n == 2:
                    keep_h(0, 3)
                act.wait_ge(filled[n % 2], X0[n % 2] + TILES + n // 2 + 1)
                weights_qkv(bank[n % 2], [w_qkv_high], n, lambda dst, src: nc.scalar.copy(dst[0], src)).then_inc(high_done[n % 2], 1)
            take(1, PREP[1] + 3, flat(w_proj[:, :, :]), bank[1][:, :])
            take(0, PREP[0] + 3, f_biasT[:, :], bank[0][:, 0:32])
            act.wait_ge(ctl_loaded, 16)
            nc.scalar.copy(ctl_high[:, :, :], ctl_sb[:, :, :]).then_inc(ctl_high_done, 1)
            take_xn(4)
            act.wait_ge(q_consts, 3)
            keys(0, 0, WIDE0, True)
            keys(0, 1, WIDE0, True)
            queries(0, WIDE0)
            queries(1, WIDE0)
            with act.Fori(0, 3) as b:
                j01, j2, j3, jw = jobs_in(b)
                ja = j01 + 4
                x_jobs = after(PREP, j01)
                take_x(0, x_jobs, j2, j3)
                take_x(1, x_jobs, j2, j3)
                exps(b, 0)
                keep_h(b + 1, 0)
                take_x(2, x_jobs, j2, j3)
                exps(b, 1)
                keep_h(b + 1, 1)
                take_x(3, x_jobs, j2, j3)
                exps(b, 2)
                probs(0, ja, jw)
                keep_h(b + 1, 2)
                exps(b, 3)
                probs(1, ja, jw)
                keep_h(b + 1, 3)
                evens(0, jw)
                probs(2, ja, jw)
                evens(1, jw)
                probs(3, ja, jw)
                evens(2, jw)
                evens(3, jw)
                take_xn(ja + 2)
                keys(b + 1, 0, jw + 1, False)
                keys(b + 1, 1, jw + 1, False)
                queries(0, jw + 1)
                queries(1, jw + 1)
                take_xn(ja + 3)
                nc.scalar.copy(batch_of(xn2, b), xn[:, :, :]).then_inc(xn2_kept, 1)
                nc.scalar.copy(batch_of(h, b), h2[:, :, :]).then_inc(h2_kept, 1)
            exps(3, 0)
            exps(3, 1)
            probs(0, L01, LW)
            exps(3, 2)
            probs(1, L01, LW)
            exps(3, 3)
            evens(0, LW)
            probs(2, L01, LW)
            evens(1, LW)
            probs(3, L01, LW)
            evens(2, LW)
            evens(3, LW)

            def take_dispatched(s, job, groups):
                for half in range(2):
                    k = 4 + 2 * s + half
                    act.wait_ge(filled[k], ENDW + job + 1)
                    nc.scalar.copy(dispT[:, half, :, groups], bank[k].rearrange("p (c e) -> p e c", c=4)).then_inc(copied[k], 1)

            for t in range(3):
                take_dispatched(t % 2, t // 2, slice(4 * t, 4 * t + 4))
            take_xn(XN_TURNED)
            take_dispatched(1, 1, slice(12, 16))
            with act.Fori(2, NT // 2) as i2:
                for s in range(2):
                    take_dispatched(s, i2, bass.ds(8 * i2 + 4 * s, 4))

            def f2_highs(n):
                part = (f2_high_a, f2_high_b)[n // 2]
                nc.scalar.copy(part[:, 8 * (n % 2):8 * (n % 2) + 8, :], f2_sb[:, 8 * n:8 * n + 8, :]).then_inc(f2_high_done, 1)

            def inner_highs(u):
                inner_slot_free(act, u)
                if u % 2 == 0:
                    act.wait_ge(copied[4 + u // 2 % 2], ENDW + 8 + u // 4 + 1)
                for j in range(4):
                    rows, place_j = diagonal(u, j)
                    nc.scalar.activation(inner_high[place_j], innerT[rows, 4 * u:4 * u + 4, :], ACT.Relu).then_inc(inner_high_done, 1)

            act.wait_ge(f2_loaded, 64)
            act.wait_ge(cur_ready, NT)
            f2_highs(0)
            f2_highs(1)
            inner_highs(0)
            inner_highs(1)
            act.wait_ge(filled[4], ENDW + 8 + 1)
            act.wait_ge(filled[5], ENDW + 8 + 1)
            f2_highs(2)
            f2_highs(3)
            for u in range(ROUND):
                take_mixed(act, nc.scalar.copy, u, 0)
                if u + 2 < ROUND:
                    inner_highs(u + 2)
                take_mixed(act, nc.scalar.copy, u, 2)
            with act.Fori(0, NT // 2) as i2:
                for s in range(2):
                    act.wait_ge(filled[2 + s], COMB0[2 + s] + i2)
                    take(4 * s, COMB0[4 * s] + i2, flat(mixed[:, s, 0:2, :]), bank[4 * s][:, :])

        @block.vector
        def _(dve):
            def low(i, n, dst, high_part):
                dve.wait_ge(high_done[i], n + 1)
                nc.vector.tensor_tensor(dst, bank[i][:, :], high_part.bitcast(F32), ALU.subtract).then_inc(copied[i], 1)

            def take_x(t, base):
                for i in range(2):
                    ks = slice(4 * i, 4 * i + 4)
                    low(i, base[i] + t, flat(xT_low[:, t % 2, ks, :]), flat(xT_high[:, t % 2, ks, :]))

            def h_stats(b, t, j2, j3):
                i, j = (2, j2) if t % 2 == 0 else (3, j3)
                dve.wait_ge(filled[i], j + t // 2 + 1)
                nc.vector.bn_stats(stat[:, t, :], bank[i][:, 0:C]).then_inc(stat_done, 1)

            def variance(b, stats, stats_done, m_v, aggregated, v_eps, added):
                dve.wait_ge(stats_done, 4 * (b + 1))
                nc.vector.memset(v_eps[:, :], EPS).then_inc(aggregated, 1)
                for t in range(TILES):
                    nc.vector.bn_aggr(m_v[:, t, :], stats[:, t, :]).then_inc(aggregated, 1)
                dve.wait_ge(aggregated, 5 * (b + 1))
                nc.vector.tensor_tensor(v_eps[:, :], m_v[:, :, 1], v_eps[:, :], ALU.add).then_inc(added, 1)

            def normalise(b, rows, m_v, inv, inv_ready, done, dst):
                dve.wait_ge(inv_ready, b + 1)
                for t in range(TILES):
                    nc.vector.tensor_scalar(dst[:, t, :], rows[:, t, :], m_v[:, t, 0:1], inv[:, t:t + 1],
                                            ALU.subtract, ALU.mult).then_inc(done, 1)

            def first_variance(b, j2, j3):
                dve.wait_ge(copied[2], j2 + 2)
                dve.wait_ge(copied[3], j3 + 2)
                variance(b, stat, stat_done, mean_var, aggr_done, var_eps, eps_added)

            def first_norm(b):
                normalise(b, h1, mean_var, rstd, rstd_ready, xn_ready, xn)

            def take_xn(n):
                for i in range(2):
                    low(i, HIGH0[i] + n, xnT_low[:, i, :], xnT_high[:, i, :])

            def value_rows(t, j2, j3):
                i, j = (2, j2) if t % 2 == 0 else (3, j3)
                dve.wait_ge(filled[i], j + t // 2 + 1)
                nc.vector.tensor_tensor(v_sb[:, t, :], bank[i][:, 0:C], v_bias[:, :], ALU.add).then_inc(copied[i], 1)

            def rows_of(t):
                return score[:, t, :, :].rearrange("p n (g r) -> p (n g) r", r=KEYS)

            def row_maxima(b, t, jw):
                dve.wait_ge(filled[4 + t], jw + 1)
                lo = 0 if t == 0 else 2 if t == 3 else 1
                nc.vector.tensor_tensor(flat(score[:, t, :, :]), bank[4 + t][:, :],
                                        flat(bias_tab[:, lo:lo + 2, :]), ALU.add).then_inc(copied[4 + t], 1)
                dve.wait_ge(copied[4 + t], jw + 1)
                nc.vector.tensor_reduce(row_max[:, t, :], rows_of(t), AX.X, ALU.max).then_inc(max_done, 1)

            def row_sums(b, t):
                dve.wait_ge(exp_done, 4 * b + t + 1)
                nc.vector.tensor_reduce(row_sum[:, t, :], rows_of(t), AX.X, ALU.add).then_inc(sum_done, 1)
                dve.wait_ge(sum_done, 4 * b + t + 1)
                nc.vector.reciprocal(row_inv[:, t, :], row_sum[:, t, :]).then_inc(inv_done, 1)

            def odds(b, t):
                dve.wait_ge(even_done, 4 * b + t + 1)
                nc.vector.scalar_tensor_tensor(
                    out=att[:, t, :, :].rearrange("p n (m d) -> p (n m) d", d=HD),
                    in0=bank[4 + t].rearrange("p (n a d) -> p n a d", a=2, d=HD)[:, :, 1, :], scalar=parity[:, 1:2],
                    in1=even[:, t % 2, :].rearrange("p (n d) -> p n d", d=HD), op0=ALU.mult, op1=ALU.add).then_inc(copied[4 + t], 1)

            def turned(t, j2, j3):
                if t >= 2:
                    dve.wait_ge(filled[3], j3 + t - 2 + 1)
                dve.wait_ge(filled[2], j2 + t + 1)
                nc.vector.tensor_copy(attT[:, t % 2, :, :].rearrange("p a (n q) -> p n a q", q=BLK),
                                      bank[2][:, 0:256].rearrange("p (n a q) -> p n a q", a=2, q=BLK)).then_inc(copied[2], 1)

            def residual(b, t, j3):
                row = h2[:, t, :] if b is not BATCH - 1 else h[:, 4 * b + t, :]
                dve.wait_ge(filled[3], j3 + t + 1)
                dve.wait_ge(h_biased, 4 * b + t + 1)
                nc.vector.tensor_tensor(row, bank[3][:, 0:C], tile_of(h, 4 * b + t), ALU.add).then_inc(copied[3], 1)
                dve.wait_ge(copied[3], j3 + t + 1)
                nc.vector.bn_stats(stat2[:, t, :], row).then_inc(stat2_done, 1)

            def second_norm(b):
                if b is not BATCH - 1:
                    normalise(b, h2, mean_var2, rstd2, rstd2_ready, xn2_ready, xn)
                else:
                    normalise(b, h[:, NT - TILES:NT, :], mean_var2, rstd2, rstd2_ready, xn2_ready, xn2[:, NT - TILES:NT, :])

            by_group = logit[:, :].rearrange("p (g t) -> p g t", t=GROUP)

            def route_ties(j2):
                dve.wait_ge(filled[2], j2 + 1)
                nc.vector.tensor_tensor(by_group, bank[2].rearrange("p (g t) -> p g t", t=GROUP),
                                        tie[:, :].unsqueeze(1).broadcast_to([P, SEQ // GROUP, GROUP]), ALU.add).then_inc(copied[2], 1)

            def route_max(j2):
                dve.wait_ge(copied[2], j2 + 1)
                nc.vector.tensor_reduce(gmax[:, :], by_group, AX.X, ALU.max).then_inc(gmax_done, 1)

            def route_pick(b):
                dve.wait_ge(gmax_done, b + 1)
                nc.vector.tensor_tensor(permT[:, bass.ds(SEQ * b, SEQ)].rearrange("p (g t) -> p g t", t=GROUP), by_group,
                                        gmax[:, :].unsqueeze(2).broadcast_to([P, SEQ // GROUP, GROUP]), ALU.is_equal).then_inc(perm_done, 1)

            nc.vector.memset(tab_fill[:, :], MASKED).then_inc(tab_masked, 1)
            nc.vector.memset(minus_half[:, :], -0.5).then_inc(half_set, 1)
            dve.wait_ge(tok_w_loaded, 32)
            quart = C // 4
            for n in range(4):
                for o in range(2):
                    cols = slice(quart * n, quart * (n + 1))
                    nc.vector.tensor_tensor(w_mix[:, o, cols, :], w_sum_sb[:, o, cols].unsqueeze(2).broadcast_to([P, quart, TAPS]),
                                            w_taps_sb[:, o, :].unsqueeze(1).broadcast_to([P, quart, TAPS]), ALU.mult).then_inc(w_mixed, 1)
            dve.wait_ge(ident_ready, 1)
            nc.vector.tensor_reduce(parity[:, :], ident[:, :].rearrange("p (c a q) -> p a c q", c=4, a=2), AX.XY, ALU.add).then_inc(masks_ready, 1)
            nc.vector.tensor_reduce(quarter[:, :], ident[:, :].rearrange("p (c q) -> p c q", c=4), AX.X, ALU.add).then_inc(masks_ready, 1)
            for n in range(4):
                ks = slice(2 * n, 2 * n + 2)
                dve.wait_ge(w_high_done, n + 1)
                nc.vector.tensor_tensor(flat(w_tok_low[:, ks, :]), bank[4 + n][:, :], flat(w_tok_high[:, ks, :]).bitcast(F32),
                                        ALU.subtract).then_inc(copied[4 + n], 1)
            def qkv_weights(n):
                dve.wait_ge(high_done[n % 2], X0[n % 2] + TILES + n // 2 + 1)
                weights_qkv(bank[n % 2], [w_qkv_low, w_qkv_high], n, lambda dst, src: nc.vector.tensor_tensor(
                    dst[0], src, dst[1].bitcast(F32), ALU.subtract)).then_inc(copied[n % 2], 1)

            for t in range(TILES):
                take_x(t, X0)
                if t:
                    h_stats(0, t - 1, 0, 0)
            qkv_weights(0)
            qkv_weights(1)
            h_stats(0, 3, 0, 0)
            first_variance(0, 0, 0)
            qkv_weights(2)
            dve.wait_ge(ctl_high_done, 1)
            nc.vector.tensor_tensor(ctl_low[:, :, :], ctl_sb[:, :, :], ctl_high[:, :, :].bitcast(F32), ALU.subtract).then_inc(ctl_split, 1)
            dve.wait_ge(masks_ready, 2)
            dve.wait_ge(vec_loaded, 80)
            nc.vector.tensor_scalar(q_scale[:, :], parity[:, :], HD ** -0.5, None, ALU.mult).then_inc(q_consts, 1)
            dve.wait_ge(q_consts, 1)
            for half in range(2):
                nc.vector.tensor_scalar(q_bias[:, half, :], q_scale[:, :], qkv_bc[:, half:half + 1], None, ALU.mult).then_inc(q_consts, 1)
            first_norm(0)
            take_xn(4)
            for t in range(TILES):
                value_rows(t, 2, 2)
            dve.wait_ge(tab_spread, 96)
            row_maxima(0, 0, WIDE0 + 1)
            with dve.Fori(0, 3) as b:
                j01, j2, j3, jw = jobs_in(b)
                n, j2a, j3a = high_in(b), j2 + 2, j3 + 2
                take_x(0, after(HIGH0, n))
                take_x(1, after(HIGH0, n))
                row_maxima(b, 1, jw - 1)
                h_stats(b + 1, 0, j2, j3)
                take_x(2, after(HIGH0, n))
                row_maxima(b, 2, jw - 1)
                h_stats(b + 1, 1, j2, j3)
                take_x(3, after(HIGH0, n))
                row_maxima(b, 3, jw - 1)
                row_sums(b, 0)
                h_stats(b + 1, 2, j2, j3)
                row_sums(b, 1)
                row_sums(b, 2)
                h_stats(b + 1, 3, j2, j3)
                odds(b, 0)
                first_variance(b + 1, j2, j3)
                row_sums(b, 3)
                odds(b, 1)
                turned(0, j2a, j3a)
                first_norm(b + 1)
                odds(b, 2)
                turned(1, j2a, j3a)
                residual(b, 0, j3a)
                odds(b, 3)
                take_xn(n + 4)
                turned(2, j2a, j3a)
                residual(b, 1, j3a)
                turned(3, j2a, j3a)
                residual(b, 2, j3a)
                residual(b, 3, j3a)
                variance(b, stat2, stat2_done, mean_var2, aggr2_done, var_eps2, eps2_added)
                dve.wait_ge(v_written, 16 * (b + 1))
                value_rows(0, j2 + 6, j3 + 6)
                value_rows(1, j2 + 6, j3 + 6)
                second_norm(b)
                value_rows(2, j2 + 6, j3 + 6)
                value_rows(3, j2 + 6, j3 + 6)
                take_xn(n + 5)
                row_maxima(b + 1, 0, jw + 2)
                route_ties(j2 + 8)
                route_max(j2 + 8)
                route_pick(b)
            for t in range(1, TILES):
                row_maxima(3, t, LW - 1)
            for t in range(TILES):
                row_sums(3, t)
                if t == 2:
                    odds(3, 0)
            odds(3, 1)
            turned(0, L2, L3)
            odds(3, 2)
            turned(1, L2, L3)
            residual(3, 0, L3)
            odds(3, 3)
            turned(2, L2, L3)
            residual(3, 1, L3)
            turned(3, L2, L3)

            def dispatch_operands(t):
                dve.wait_ge(x_high_done, t + 1)
                nc.vector.tensor_tensor(x_cur_low[:, t % 4, :], xn2[:, t, :], x_cur_high[:, t % 4, :].bitcast(F32),
                                        ALU.subtract).then_inc(cur_ready, 1)
                dve.wait_ge(filled[t % 2], perm_job(t) + 1)
                if t >= 2:
                    dve.wait_ge(filled[5 + 2 * (t % 2)], ENDW + t // 2)
                nc.vector.tensor_tensor(perm_bd[:, t % 2, :, :], bank[t % 2][:, 0:P].unsqueeze(1).broadcast_to([P, 4, P]),
                                        quarter[:, :].unsqueeze(2).broadcast_to([P, 4, P]), ALU.mult).then_inc(copied[t % 2], 1)

            dispatch_operands(0)
            residual(3, 2, L3)
            dispatch_operands(1)
            residual(3, 3, L3)
            variance(3, stat2, stat2_done, mean_var2, aggr2_done, var_eps2, eps2_added)
            dispatch_operands(2)
            second_norm(3)
            dispatch_operands(3)
            take_xn(high_in(3))
            for t in range(4, 7):
                dispatch_operands(t)
            route_ties(L2 + 4)
            dispatch_operands(7)
            route_max(L2 + 4)
            dispatch_operands(8)
            route_pick(3)
            for t in range(9, NT):
                dispatch_operands(t)
            def inner_lows(u):
                inner_slot_free(dve, u)
                for j in range(4):
                    rows, place_j = diagonal(u, j)
                    dve.wait_ge(inner_high_done, 4 * u + j + 1)
                    nc.vector.scalar_tensor_tensor(out=inner_low[place_j], in0=innerT[rows, 4 * u:4 * u + 4, :], scalar=0.0,
                                                   in1=inner_high[place_j].bitcast(F32), op0=ALU.max, op1=ALU.subtract).then_inc(inner_split, 1)

            for rnd in range(4):
                qs = slice(8 * rnd, 8 * rnd + 8)
                if rnd < 2:
                    f2_lows(dve, nc.vector, rnd, f2_split_v)
                i = 4 + rnd % 2
                dve.wait_ge(filled[i], ENDW + 8 + rnd // 2 + 1)
                nc.vector.tensor_tensor(innerT[:, qs, :], bank[i].rearrange("p (g n) -> p g n", g=ROUND),
                                        f_biasT[:, qs].unsqueeze(2).broadcast_to([P, ROUND, NG]),
                                        ALU.add).then_inc(copied[i], 1)
                if rnd in (1, 2):
                    inner_lows(rnd - 1)
            for u in range(ROUND):
                take_mixed(dve, nc.vector.tensor_copy, u, 1)
                if u + 2 < ROUND:
                    inner_lows(u + 2)
                take_mixed(dve, nc.vector.tensor_copy, u, 3)

            def take_turned(s, job):
                k = s % 2
                dve.wait_ge(filled[2 + k], COMB0[2 + k] + job)
                dve.wait_ge(filled[4 * k + 1], COMB0[4 * k + 1] + job + 1)
                nc.vector.tensor_copy(flat(mixed[:, k, 2:4, :]), bank[4 * k + 1][:, :]).then_inc(copied[4 * k + 1], 1)

            def add_experts(s, tile, job, stored):
                k = s % 2
                dve.wait_ge(filled[2 + k], COMB0[2 + k] + job + 1)
                if stored is not None:
                    dve.wait_ge(y_stored[s], stored)
                nc.vector.tensor_tensor(y_sb[:, s, :], bank[2 + k][:, 0:C], tile_of(h, tile), ALU.add).then_inc(copied[2 + k], 1)

            take_turned(0, 0)
            for t in range(4):
                take_turned((t + 1) % 4, (t + 1) // 2)
                add_experts(t, t, t // 2, None)
            with dve.Fori(1, NT // 4 - 1) as i4:
                for s in range(4):
                    take_turned((s + 1) % 4, 2 * i4 + (s + 1) // 2)
                    add_experts(s, 4 * i4 + s, 2 * i4 + s // 2, 16 * i4)
            for t in range(NT - 4, NT):
                if t + 1 < NT:
                    take_turned((t + 1) % 4, (t + 1) // 2)
                add_experts(t % 4, t, t // 2, 16 * (t // 4))

        @block.gpsimd
        def _(pool):
            nc.gpsimd.memset(ident[:, :], 0.0).then_inc(ident_zero, 1)
            pool.wait_ge(ident_zero, 1)
            nc.gpsimd.affine_select(out=ident[:, :], in_=ident[:, :], compare_op=ALU.not_equal, fill=1.0, base=0,
                                    pattern=[[-1, P]], channel_multiplier=1).then_inc(ident_ready, 1)

            def power(b, sem_in, src, dst, sem_out):
                pool.wait_ge(sem_in, b + 1)
                nc.gpsimd.tensor_tensor(dst[:, :], src[:, :], minus_half[:, :], ALU.pow).then_inc(sem_out, 1)

            def add_bias(b):
                for t in range(TILES):
                    nc.gpsimd.tensor_tensor(tile_of(h, 4 * b + t), h1[:, t, :], p_bias[:, :], ALU.add).then_inc(h_biased, 1)

            def shift(b, t):
                pool.wait_ge(max_done, 4 * b + t + 1)
                rows = score[:, t, :, :].rearrange("p n (g r) -> p (n g) r", r=KEYS)
                nc.gpsimd.tensor_tensor(rows, rows, row_max[:, t, :].unsqueeze(2).broadcast_to([P, 16, KEYS]),
                                        ALU.subtract).then_inc(shifted, 1)

            def scale(b, t, jw):
                pool.wait_ge(copied[4 + t], jw + 1)
                pool.wait_ge(inv_done, 4 * b + t + 1)
                rows = att[:, t, :, :].rearrange("p n (m d) -> p (n m) d", d=HD)
                nc.gpsimd.tensor_tensor(rows, rows, row_inv[:, t, :].unsqueeze(2).broadcast_to([P, 16, HD]),
                                        ALU.mult).then_inc(att_scaled, 1)

            pool.wait_ge(half_set, 1)
            power(0, eps_added, var_eps, rstd, rstd_ready)
            pool.wait_ge(copied[0], PREP[0] + TILES)
            pool.wait_ge(copied[1], PREP[1] + TILES)
            nc.gpsimd.memset(v_bd[:, :, :, :, :], 0.0).then_inc(bd_zeroed, 1)
            pool.wait_ge(vec_loaded, 80)
            pool.wait_ge(ctl_split, 1)
            pool.wait_ge(tab_loaded, 16)
            nc.gpsimd.memset(k_bd[:, :, :, :], 0.0).then_inc(bd_zeroed, 1)
            add_bias(0)
            with pool.Fori(0, 3) as b:
                j01, j2, j3, jw = jobs_in(b)
                for t in range(TILES):
                    shift(b, t)
                scale(b, 0, jw)
                power(b + 1, eps_added, var_eps, rstd, rstd_ready)
                for t in range(1, TILES):
                    scale(b, t, jw)
                add_bias(b + 1)
                power(b, eps2_added, var_eps2, rstd2, rstd2_ready)
            for t in range(TILES):
                shift(3, t)

            def high_part(t):
                if t >= 4:
                    pool.wait_ge(filled[5 + 2 * (t % 2)], ENDW + (t - 4) // 2 + 1)
                nc.gpsimd.tensor_copy(x_cur_high[:, t % 4, :], xn2[:, t, :]).then_inc(x_high_done, 1)

            pool.wait_ge(filled[7], LW)
            pool.wait_ge(v_written, 16 * BATCH)
            pool.wait_ge(xn2_kept, BATCH - 1)
            high_part(0)
            high_part(1)
            for t in range(TILES):
                scale(3, t, LW)
            high_part(2)
            high_part(3)
            power(3, eps2_added, var_eps2, rstd2, rstd2_ready)
            for t in range(4, NT):
                if t == NT - TILES:
                    pool.wait_ge(xn2_ready, 4 * BATCH)
                high_part(t)
            pool.wait_ge(perm_done, BATCH)
            nc.gpsimd.memset(inner_high[:, :, :, :, :].bitcast(F32), 0.0).then_inc(inner_zeroed, 1)
            for k in range(4, 8):
                pool.wait_ge(filled[k], ENDW + 8)
            nc.gpsimd.memset(inner_low[:, :, :, :, :].bitcast(F32), 0.0).then_inc(inner_zeroed, 1)
            for n in (2, 3):
                f2_lows(pool, nc.gpsimd, n, f2_split_p)


_IN = ["x", "L0_tok_weight", "L0_tok_weighted_sum", "L0_attn_qkv_w", "L0_attn_qkv_b", "L0_attn_rpb", "L0_attn_proj_w",
       "L0_attn_proj_b", "L0_ffn_controller", "L0_ffn_f1", "L0_ffn_bias", "L0_ffn_f2"]


def kernel(**inputs):
    import concourse.bacc as bacc
    from concourse.bass_utils import run_bass_kernel_spmd

    nc = bacc.Bacc("TRN2", target_bir_lowering=False, num_devices=1, dynamic_dma_scratch_size=1024)
    arrays, args = {}, []
    arrays["ties"] = np.float32(1e-6) / np.float32(GROUP - 1) * np.arange(GROUP, dtype=np.float32)
    for name in _IN:
        arrays[name] = np.ascontiguousarray(inputs[name])
        args.append(nc.dram_tensor(name, arrays[name].shape, mybir.dt.from_np(arrays[name].dtype), kind="ExternalInput").ap())
    args.append(nc.dram_tensor("ties", (GROUP,), F32, kind="ExternalInput").ap())
    args.append(nc.dram_tensor("out", (BATCH, SEQ, C), F32, kind="ExternalOutput").ap())
    build(nc, *args)
    r = run_bass_kernel_spmd(nc, [arrays], core_ids=[0])
    return r.results[0]["out"]
```
